# Optimizing a Trainium2 kernel written in Bass

```python
import numpy as np
import jax
import jax.numpy as jnp

def _softmax(x, axis=-1):
    return jax.nn.softmax(x, axis=axis)
def _gelu(x):
    return jax.nn.gelu(x, approximate=True)
def _silu(x):
    return jax.nn.silu(x)
def _sigmoid(x):
    return jax.nn.sigmoid(x)
def _layernorm(x, axis=-1, eps=1e-5):
    m = jnp.mean(x, axis=axis, keepdims=True)
    v = jnp.var(x, axis=axis, keepdims=True)
    return (x - m) / jnp.sqrt(v + eps)
def _scatter_add(tgt, idx, src, axis=0):
    return tgt.at[idx].add(src)
def _segment_sum(src, seg, n):
    return jax.ops.segment_sum(src, seg, n)

kernel_name = 'mk_conv_seq_d1_conv_nhwc512_0f6552'

def setup_inputs(seed: int = 0):
    np.random.seed(seed)
    _w = jnp.asarray
    def _rec_inputs():
        import jax
        import jax.numpy as jnp
        _gk = jax.random.key(seed)
        x = -0.0001748 + 1 * jax.random.normal(jax.random.fold_in(_gk, 1), (16, 30, 30, 512), jnp.float32)
        return x
    x = _rec_inputs()
    def _L0_conv_setup():
        import jax, jax.numpy as jnp
        import numpy as np
        D_MODEL = 512
        NUM_HEADS = 8
        BIAS_SIZE = 2 * 30 - 1
        LN_EPS = 1e-05

        def _spatial_bias_matrix(spatial_bias, H, W):
            idx = jnp.arange(H * W)
            hh, ww = (idx // W, idx % W)
            dist = jnp.abs(hh[:, None] - hh[None, :]) + jnp.abs(ww[:, None] - ww[None, :])
            return spatial_bias[:, 0][dist]
        key = jax.random.key(seed)
        ks = jax.random.split(key, 12)
        d = D_MODEL
        s = 1.0 / np.sqrt(d)
        inp = {'x': jax.random.normal(ks[0], (16, 30, 30, d), dtype=jnp.float32), 'wq': jax.random.normal(ks[1], (d, d), dtype=jnp.float32) * s, 'bq': jnp.zeros((d,), jnp.float32), 'wk': jax.random.normal(ks[2], (d, d), dtype=jnp.float32) * s, 'bk': jnp.zeros((d,), jnp.float32), 'wv': jax.random.normal(ks[3], (d, d), dtype=jnp.float32) * s, 'bv': jnp.zeros((d,), jnp.float32), 'wo': jax.random.normal(ks[4], (d, d), dtype=jnp.float32) * s, 'bo': jnp.zeros((d,), jnp.float32), 'ln_gamma': jnp.ones((d,), jnp.float32), 'ln_beta': jnp.zeros((d,), jnp.float32), 'spatial_bias': jax.random.normal(ks[5], (BIAS_SIZE, BIAS_SIZE), dtype=jnp.float32) * 0.02}
        return inp
    _L0_conv_all = _L0_conv_setup()
    _L0_conv_in = {k: v for k, v in _L0_conv_all.items() if k in ('wq', 'bq', 'wk', 'bk', 'wv', 'bv', 'wo', 'bo', 'ln_gamma', 'ln_beta', 'spatial_bias', )}
    del _L0_conv_all

    return {
        "x": x,
        "L0_conv_wq": _L0_conv_in["wq"],
        "L0_conv_bq": _L0_conv_in["bq"],
        "L0_conv_wk": _L0_conv_in["wk"],
        "L0_conv_bk": _L0_conv_in["bk"],
        "L0_conv_wv": _L0_conv_in["wv"],
        "L0_conv_bv": _L0_conv_in["bv"],
        "L0_conv_wo": _L0_conv_in["wo"],
        "L0_conv_bo": _L0_conv_in["bo"],
        "L0_conv_ln_gamma": _L0_conv_in["ln_gamma"],
        "L0_conv_ln_beta": _L0_conv_in["ln_beta"],
        "L0_conv_spatial_bias": _L0_conv_in["spatial_bias"],
    }

def reference(x, L0_conv_wq, L0_conv_bq, L0_conv_wk, L0_conv_bk, L0_conv_wv, L0_conv_bv, L0_conv_wo, L0_conv_bo, L0_conv_ln_gamma, L0_conv_ln_beta, L0_conv_spatial_bias):
    import jax
    import jax.numpy as jnp
    def _L0_conv_ref(x, wq, bq, wk, bk, wv, bv, wo, bo, ln_gamma, ln_beta, spatial_bias):
        import jax, jax.numpy as jnp
        import numpy as np
        D_MODEL = 512
        NUM_HEADS = 8
        BIAS_SIZE = 2 * 30 - 1
        LN_EPS = 1e-05

        def _spatial_bias_matrix(spatial_bias, H, W):
            idx = jnp.arange(H * W)
            hh, ww = (idx // W, idx % W)
            dist = jnp.abs(hh[:, None] - hh[None, :]) + jnp.abs(ww[:, None] - ww[None, :])
            return spatial_bias[:, 0][dist]
        B, H, W, d_model = x.shape
        S = H * W
        d_k = d_model // NUM_HEADS
        x_seq = x.reshape(B, S, d_model)

        def proj(w, b):
            return (x_seq @ w + b).reshape(B, S, NUM_HEADS, d_k).transpose(0, 2, 1, 3)
        q = proj(wq, bq)
        k = proj(wk, bk)
        v = proj(wv, bv)
        scores = jnp.einsum('bhqd,bhkd->bhqk', q, k) / jnp.sqrt(jnp.float32(d_k))
        scores = scores + _spatial_bias_matrix(spatial_bias, H, W)[None, None]
        attn = jax.nn.softmax(scores, axis=-1)
        ctx = jnp.einsum('bhqk,bhkd->bhqd', attn, v)
        ctx = ctx.transpose(0, 2, 1, 3).reshape(B, S, d_model)
        out = ctx @ wo + bo
        resid = out + x_seq
        mu = jnp.mean(resid, axis=-1, keepdims=True)
        var = jnp.mean((resid - mu) ** 2, axis=-1, keepdims=True)
        out = (resid - mu) * jax.lax.rsqrt(var + LN_EPS) * ln_gamma + ln_beta
        return out.reshape(B, H, W, d_model)

    def _gn(v, G=32, eps=1e-5):
        B_, H_, W_, C_ = v.shape
        g = v.reshape(B_, H_, W_, G, C_ // G)
        m = jnp.mean(g, axis=(1, 2, 4), keepdims=True)
        s = jnp.var(g, axis=(1, 2, 4), keepdims=True)
        return ((g - m) / jnp.sqrt(s + eps)).reshape(v.shape)

    def _ln_c(v, eps=1e-6):
        m = jnp.mean(v, axis=-1, keepdims=True)
        s = jnp.var(v, axis=-1, keepdims=True)
        return (v - m) / jnp.sqrt(s + eps)

    def _ln_t(v, eps=1e-5):
        m = jnp.mean(v, axis=-1, keepdims=True)
        s = jnp.var(v, axis=-1, keepdims=True)
        return (v - m) / jnp.sqrt(s + eps)

    def _to_tokens(v):
        B_, H_, W_, C_ = v.shape
        return v.reshape(B_, H_ * W_, C_)
    def _from_tokens(t, like):
        return t.reshape(like.shape)

    x = _L0_conv_ref(x, L0_conv_wq, L0_conv_bq, L0_conv_wk, L0_conv_bk, L0_conv_wv, L0_conv_bv, L0_conv_wo, L0_conv_bo, L0_conv_ln_gamma, L0_conv_ln_beta, L0_conv_spatial_bias)
    return x


_drawn_inputs = setup_inputs


def setup_inputs(seed=0):
    import zlib

    import numpy as np

    out = dict(_drawn_inputs(seed))
    spreads = {'L0_conv_bq': (0.0, 0.8),
     'L0_conv_bk': (0.0, 2.0),
     'L0_conv_bv': (0.0, 0.1),
     'L0_conv_bo': (0.0, 0.1),
     'L0_conv_ln_gamma': (1.0, 0.2),
     'L0_conv_ln_beta': (0.0, 0.1)}
    factors = {'L0_conv_spatial_bias': 39.002}
    for name, (base, spread) in spreads.items():
        noise = np.random.default_rng([zlib.crc32(name.encode()), seed]).standard_normal(out[name].shape)
        drawn = base * np.exp(spread * noise) if base else spread * noise
        out[name] = jnp.asarray(drawn.astype(out[name].dtype))
    for name, factor in factors.items():
        out[name] = (out[name] * factor).astype(out[name].dtype)
    return out
```

```python
from contextlib import ExitStack

import concourse.bass as bass
from concourse import mybir

F32 = mybir.dt.float32
F32R = mybir.dt.float32r
ALU = mybir.AluOpType
ACT = mybir.ActivationFunctionType

B, GRID, D, HEADS = 16, 30, 512, 8
S = GRID * GRID
DK = D // HEADS
ROWS = 4
TT = ROWS * GRID
NT = -(-S // TT)
SP_ = NT * TT
LAST = S - (NT - 1) * TT
HALF = S // 2
KT = D // 128
PAIRS = HEADS // 2
UNITS = PAIRS * NT * 2
PER_PAIR = NT * 2
GROUPS = PAIRS * NT // 2
PER_GROUP = 4
GW = 2 * TT
BIAS = 2 * GRID - 1
WIN = 2 * NT * ROWS - ROWS - 2
EPS = 1e-5
BIG = 3.0e38
PARTS = 3
TERMS = [(0, 0), (0, 1), (1, 0)]
QUERY, KEY = 0, 1
AHEAD = 3
BUFS = 4
PIECES = [(KEY, 0), (KEY, 1), (QUERY, 0), (QUERY, 1)]


def background(u, first, last):
    work = []
    p, v = divmod(u, PER_PAIR)
    if p == 0:
        if v < NT // 2:
            work += [("value", 2 * v), ("value", 2 * v + 1)]
        if v % 2 and not first:
            work += [("out", v // 2)]
        if v in (6, 8, 10, 12):
            work += [("piece", 1, (v - 6) // 2)]
    elif p < PAIRS - 1:
        if v in (2, 5, 8, 11):
            work += [("piece", p + 1, (v - 2) // 3)]
    elif not last:
        if v < NT:
            work += [("xt", v)]
        if v in (9, 10, 11, 12):
            work += [("piece", 0, v - 9)]
    return work


PROLOGUE = [("xt", t) for t in range(NT)] + [("piece", 0, j) for j in range(len(PIECES))]


def spare_uses(first):
    uses = [w for u in range(UNITS) for w in background(u, first, False)]
    return [w for w in uses if not (w[0] == "value" and w[1] % 2)]


USES_FIRST, USES = spare_uses(True), spare_uses(False)
HIS = 2 * PAIRS * len(PIECES) + NT


def split_parts(uses):
    return sum(2 if w[0] == "piece" else 1 if w[0] == "xt" else 0 for w in uses)


class Image:

    def __init__(self, b, first=False, last=False):
        self.b, self.first, self.last = b, first, last
        self.uses = USES_FIRST if first else USES
        self.spare0 = len(PROLOGUE) + (0 if first else (b - 1) * len(USES) + len(USES_FIRST))
        self.hi0 = split_parts(PROLOGUE) + b * HIS

    def spare(self, work):
        return self.spare0 + self.uses.index(work)

    def hi(self, work):
        return self.hi0 + split_parts(self.uses[:self.uses.index(work)])

    def unit(self, u):
        return self.b * UNITS + u


class Prologue:
    b, first, last = -1, True, False

    def spare(self, work):
        return PROLOGUE.index(work)

    def hi(self, work):
        return split_parts(PROLOGUE[:PROLOGUE.index(work)])


def images(eng, body, epilogue=None):
    body(Image(0, first=True))
    with eng.Fori(1, B - 1) as b:
        body(Image(b))
    body(Image(B - 1, last=True))


def attention_layernorm(nc, x, wq, bq, wk, bk, wv, bv, wo, bo, gamma, beta, spatial_bias, out):
    x_t = x.rearrange("b h w d -> b (h w) d")
    out_t = out.rearrange("b h w d -> b (h w) d")

    with ExitStack() as ctx:
        def sb(name, shape, dt=F32):
            return ctx.enter_context(nc.sbuf_tensor(name, shape, dt))

        def sem(name):
            return ctx.enter_context(nc.semaphore(name))

        def dram(name, shape, dt):
            return nc.dram_tensor(name, shape, dt, kind="Internal").ap()

        wqk_split = dram("wqk_split", [PAIRS, 128, 2, 2, KT, 128], F32)
        bias_grid = dram("bias_grid", [BIAS + 2, BIAS], F32)
        bias_by_w = dram("bias_by_w", [GRID, BIAS + 2, GRID], F32)

        wqk_sb = sb("wqk_sb", [128, 2, KT, 128], F32R)
        wv_sb = sb("wv_sb", [128, 2, KT, D], F32R)
        wo_sb = sb("wo_sb", [128, 2, KT, D], F32R)
        window = sb("window", [TT, WIN, GRID])
        xt = sb("xt", [128, 2, KT, SP_], F32R)
        values = sb("values", [128, NT, D])
        q_sb = sb("q_sb", [128, 2, 2, SP_], F32R)
        k_sb = sb("k_sb", [128, 2, 2, 2, S], F32R)
        prob = sb("prob", [TT, BUFS, SP_])
        prob_t = sb("prob_t", [TT, 2, NT, GW])
        ctx_t = sb("ctx_t", [128, 2, PAIRS, SP_], F32R)
        tokens = sb("tokens", [TT, 2, D])
        x_nat = y = tokens
        bv_all = sb("bv_all", [TT, D])
        bo_all = sb("bo_all", [TT, D])
        gamma_all = sb("gamma_all", [TT, D])
        beta_all = sb("beta_all", [TT, D])
        bq_col = sb("bq_col", [128, PAIRS])
        bk_col = sb("bk_col", [128, PAIRS])
        ident = sb("ident", [128, 128])
        row_min = sb("row_min", [TT, 4])
        row_sum = sb("row_sum", [TT, 4])
        row_inv = sb("row_inv", [TT, 4])
        stats = sb("stats", [TT, 2, 6])
        mean_var = sb("mean_var", [TT, 2, 2])
        var_eps = sb("var_eps", [TT, 2])
        rstd = sb("rstd", [TT, 2])
        minus_half = sb("minus_half", [TT, 1])
        eps_col = sb("eps_col", [TT, 1])
        line_raw = sb("line_raw", [1, BIAS])
        grid = prob_t[0:1, :, :, :].rearrange("p h a b -> p (h a b)")[:, 0:(BIAS + 2) * BIAS]

        s_ps = ctx.enter_context(nc.psum_tensor("s_ps", [128, 2, 2, 512], F32))
        t_ps = ctx.enter_context(nc.psum_tensor("t_ps", [128, 2, 512], F32))
        pv_ps = ctx.enter_context(nc.psum_tensor("pv_ps", [128, 512], F32))
        spare_ps = ctx.enter_context(nc.psum_tensor("spare_ps", [128, 512], F32))

        wqk_raw = sem("wqk_raw")
        wvo_raw = sem("wvo_raw")
        w_hi = sem("w_hi")
        w_lo = sem("w_lo")
        wqk_kept = sem("wqk_kept")
        small_in = sem("small_in")
        bq_scaled = sem("bq_scaled")
        line_in = sem("line_in")
        grid_made = sem("grid_made")
        grid_kept = sem("grid_kept")
        by_w_kept = sem("by_w_kept")
        window_in = sem("window_in")
        cleared = sem("cleared")
        ident_zero = sem("ident_zero")
        ident_ok = sem("ident_ok")
        scores_full = sem("scores_full")
        scores_min = sem("scores_min")
        exp_done = sem("exp_done")
        inv_done = sem("inv_done")
        prob_done = sem("prob_done")
        t0_full = sem("t0_full")
        t1_full = sem("t1_full")
        t0_moved = sem("t0_moved")
        t1_moved = sem("t1_moved")
        pv_full = sem("pv_full")
        ctx_hi = sem("ctx_hi")
        ctx_lo = sem("ctx_lo")
        spare_full = sem("spare_full")
        spare_hi = sem("spare_hi")
        spare_lo_a = sem("spare_lo_a")
        spare_free = sem("spare_free")
        odd_value_full = sem("odd_value_full")
        odd_value_free = sem("odd_value_free")
        x_in = [sem(f"x_in{i}") for i in range(2)]
        wqk_in = sem("wqk_in")
        k_copied = sem("k_copied")
        res_in = [sem(f"res_in{i}") for i in range(2)]
        res_bias = sem("res_bias")
        res_sum = sem("res_sum")
        stats_done = sem("stats_done")
        mean_done = sem("mean_done")
        eps_done = sem("eps_done")
        rstd_done = sem("rstd_done")
        normed = sem("normed")
        scaled = sem("scaled")
        shifted = sem("shifted")
        stored = [sem(f"stored{i}") for i in range(2)]

        block = ctx.enter_context(nc.Block())

        def rows(t):
            return LAST if t == NT - 1 else TT

        def halves(ap):
            return ap.rearrange("p (a c) -> p a c", a=2)

        @block.sync
        def _(sp):
            raw = [values[:, 0:KT, :], values[:, KT:2 * KT, :]]

            sp.dma_start(line_raw[:, :], spatial_bias[:, 0:1].rearrange("a b -> b a"),
                         allow_slow_non_contiguous=True).then_inc(line_in, 16)
            for r, w in zip(raw, (wq, wk)):
                sp.dma_start(r, w.rearrange("(t p) n -> p t n", p=128)).then_inc(wqk_raw, 16)
            sp.dma_start(bq_col[:, :], bq.rearrange("(t p) -> p t", p=128), allow_slow_non_contiguous=True).then_inc(small_in, 16)
            sp.dma_start(bk_col[:, :], bk.rearrange("(t p) -> p t", p=128), allow_slow_non_contiguous=True).then_inc(small_in, 16)
            for dst, src in ((bv_all, bv), (bo_all, bo), (gamma_all, gamma), (beta_all, beta)):
                sp.dma_start(dst[:, :], src.rearrange("(a d) -> a d", a=1).broadcast_to([TT, D])
                             ).then_inc(small_in, 16)

            def load_x(b, t):
                sp.dma_start(x_nat[0:rows(t), t % 2, :], x_t[b, t * TT:t * TT + rows(t), :]
                             ).then_inc(x_in[t % 2], 16)

            for t in range(2):
                load_x(0, t)

            sp.wait_ge(grid_made, 5)
            sp.dma_start(bias_grid, grid).then_inc(grid_kept, 16)
            sp.wait_ge(grid_kept, 16)
            for w in range(GRID):
                sp.dma_start(bias_by_w[w], bias_grid[:, GRID - 1 - w:2 * GRID - 1 - w]).then_inc(by_w_kept, 16)
            sp.wait_ge(by_w_kept, 16 * GRID)
            for hh in range(ROWS):
                r0 = ROWS - 1 - hh
                sp.dma_start(window[hh * GRID:(hh + 1) * GRID, :, :], bias_by_w[:, r0:r0 + WIN, :]
                             ).then_inc(window_in, 16)

            sp.wait_ge(w_lo, 2)
            for kind, src in ((QUERY, xt), (KEY, ctx_t)):
                for part in range(2):
                    for p in range(PAIRS):
                        sp.dma_start(wqk_split[p, :, kind, part, :, :],
                                     src[:, part, :, 128 * p:128 * p + 128].bitcast(F32)
                                     ).then_inc(wqk_kept, 16)
            for r, w in zip(raw, (wv, wo)):
                sp.dma_start(r, w.rearrange("(t p) n -> p t n", p=128)).then_inc(wvo_raw, 16)
            sp.wait_ge(wqk_kept, 16 * 4 * PAIRS)

            def load_wqk(p, kind):
                sp.dma_start(wqk_sb[:, :, :, :].bitcast(F32), wqk_split[p, :, kind]).then_inc(wqk_in, 16)

            load_wqk(0, KEY)

            def copy_keys(im, p, j):
                sp.wait_ge(spare_free, im.spare(("piece", p, j)) + 1)
                cols = slice(PIECES[j][1] * HALF, PIECES[j][1] * HALF + HALF)
                for head in range(2):
                    a, c = DK * head, DK * (1 - head)
                    sp.dma_start(k_sb[c:c + DK, p % 2, head, :, cols].bitcast(F32),
                                 k_sb[a:a + DK, p % 2, head, :, cols].bitcast(F32)
                                 ).then_inc(k_copied, 16)

            def after_piece(im, p, j, more=True):
                if PIECES[j][1] and more:
                    sp.wait_ge(spare_full, im.spare(("piece", p, j)) + 1)
                    load_wqk(*((p, QUERY) if PIECES[j][0] == KEY else ((p + 1) % PAIRS, KEY)))
                if PIECES[j][0] == KEY:
                    copy_keys(im, p, j)

            pro = Prologue()
            for t in range(2, NT):
                sp.wait_ge(spare_full, pro.spare(("xt", t - 2)) + 1)
                load_x(0, t)
            for j in range(len(PIECES)):
                after_piece(pro, 0, j)

            def load_residual(b, t):
                sp.dma_start(y[0:rows(t), t % 2, :], x_t[b, t * TT:t * TT + rows(t), :]
                             ).then_inc(res_in[t % 2], 16)

            def store(b, t):
                sp.wait_ge(shifted, NT * b + t + 1)
                sp.dma_start(out_t[b, t * TT:t * TT + rows(t), :], y[0:rows(t), t % 2, :]
                             ).then_inc(stored[t % 2], 16)
                if t + 2 < NT:
                    sp.wait_ge(stored[t % 2], 16 * (NT // 2 * b + t // 2 + 1))
                    load_residual(b, t + 2)

            def first_residuals(b):
                for t in range(2):
                    load_residual(b, t)

            def body(im):
                for u in range(UNITS):
                    if u == 0 and not im.first:
                        first_residuals(im.b - 1)
                    if not im.first and 3 <= u < 3 + 2 * NT and u % 2:
                        store(im.b - 1, (u - 3) // 2)
                    if u and not (im.first and u == 0):
                        for work in background(u - 1, im.first, im.last):
                            if work[0] == "piece":
                                p = work[1]
                                after_piece(im, p, work[2], not (im.last and p == PAIRS - 1 and work[2] == 3))
                    if not im.last:
                        if u == UNITS - PER_PAIR - 6:
                            for t in range(2):
                                if im.first:
                                    sp.wait_ge(spare_full, len(PROLOGUE))
                                else:
                                    sp.wait_ge(stored[t], 16 * (NT // 2) * im.b)
                                    sp.nop(nofuse=True)
                                load_x(im.b + 1, t)
                        v = u - (UNITS - PER_PAIR)
                        if 1 <= v <= NT - 2:
                            sp.wait_ge(spare_full, im.spare(("xt", v - 1)) + 1)
                            load_x(im.b + 1, v + 1)
                        if v == NT:
                            sp.wait_ge(spare_full, im.spare(("xt", NT - 1)) + 1)
                            sp.nop(nofuse=True)

            images(sp, body)
            for i in range(2):
                sp.wait_ge(stored[i], 16 * (NT // 2) * (B - 1))
            first_residuals(B - 1)
            for t in range(NT):
                store(B - 1, t)
            for i in range(2):
                sp.wait_ge(stored[i], 16 * (NT // 2) * B)

        @block.tensor
        def _(pe):
            def xt_tile(im, t):
                n = im.spare(("xt", t))
                if not isinstance(n, int) or n:
                    pe.wait_ge(spare_free, n)
                pe.wait_ge(x_in[t % 2], 16 * (NT // 2 * (im.b + 1) + t // 2 + 1))
                for k in range(KT):
                    last = pe.transpose(spare_ps[:, k * TT:k * TT + TT], x_nat[:, t % 2, 128 * k:128 * k + 128],
                                        ident[0:TT, 0:TT])
                last.then_inc(spare_full, 1)

            def piece(im, p, j):
                kind, half = PIECES[j]
                pe.wait_ge(spare_free, im.spare(("piece", p, j)))
                if half == 0:
                    pe.wait_ge(wqk_in, 32 * (PAIRS * (im.b + 1 if p == 0 else im.b) + p) + (16 if kind == KEY else 32))
                for k in range(KT):
                    for i, (a, c) in enumerate(TERMS):
                        last = pe.matmul(spare_ps[:, 0:HALF], wqk_sb[:, a, k, :],
                                         xt[:, c, k, half * HALF:half * HALF + HALF],
                                         start=(k == 0 and i == 0), stop=(k == KT - 1 and i == PARTS - 1))
                last.then_inc(spare_full, 1)

            def value_tile(im, t):
                if t % 2 == 0:
                    pe.wait_ge(spare_free, im.spare(("value", t)))
                    if t == 0 and im.first:
                        pe.wait_ge(w_lo, 4)
                elif t == 1:
                    if not im.first:
                        pe.wait_ge(ctx_lo, GROUPS * im.b)
                else:
                    pe.wait_ge(odd_value_free, NT // 2 * im.b + t // 2)
                bank = pv_ps if t % 2 else spare_ps
                for k in range(KT):
                    for i, (a, c) in enumerate(TERMS):
                        last = pe.matmul(bank[0:TT, :], xt[:, a, k, t * TT:t * TT + TT], wv_sb[:, c, k, :],
                                         start=(k == 0 and i == 0), stop=(k == KT - 1 and i == PARTS - 1))
                last.then_inc(odd_value_full if t % 2 else spare_full, 1)

            def out_tile(n, b, t):
                pe.wait_ge(spare_free, n)
                if t == 0:
                    pe.wait_ge(ctx_lo, GROUPS * (b + 1))
                for k in range(PAIRS):
                    for i, (a, c) in enumerate(TERMS):
                        last = pe.matmul(spare_ps[0:TT, :], ctx_t[:, a, k, t * TT:t * TT + TT], wo_sb[:, c, k, :],
                                         start=(k == 0 and i == 0), stop=(k == PAIRS - 1 and i == PARTS - 1))
                last.then_inc(spare_full, 1)

            def scores(im, u, pieces_of):
                p, v = divmod(u % UNITS, PER_PAIR)
                t, head = divmod(v, 2)
                unit = im.unit(u)
                if v == 0:
                    pe.wait_ge(spare_free, pieces_of.spare(("piece", p, len(PIECES) - 1)) + 1)
                    pair = PAIRS * im.b + u // PER_PAIR
                    pe.wait_ge(k_copied, 64 * (pair + 1))
                if not isinstance(unit, int) or unit >= 2:
                    pe.wait_ge(scores_min, unit - 1)
                for half in range(2):
                    for part in range(2):
                        last = pe.matmul(s_ps[0:TT, u % 2, half, 0:HALF],
                                         q_sb[:, p % 2, head, t * TT:t * TT + TT],
                                         k_sb[:, p % 2, head, part, half * HALF:half * HALF + HALF],
                                         start=(part == 0), stop=(part == 1))
                last.then_inc(scores_full, 1)

            def transposes(im, u):
                unit = im.unit(u)
                pe.wait_ge(prob_done, unit + 1)
                if not isinstance(unit, int) or unit:
                    pe.wait_ge(t0_moved, unit)
                    pe.wait_ge(t1_moved, unit)
                for k in range(NT):
                    last = pe.transpose(t_ps[0:TT, k // 4, k % 4 * TT:k % 4 * TT + TT],
                                        prob[:, u % BUFS, k * TT:k * TT + TT], ident[0:TT, 0:TT])
                    if k == 3:
                        last.then_inc(t0_full, 1)
                last.then_inc(t1_full, 1)

            def context(im, g):
                group = GROUPS * im.b + g
                pe.wait_ge(t0_moved, PER_GROUP * (group + 1))
                pe.wait_ge(t1_moved, PER_GROUP * (group + 1))
                if g == 0:
                    pe.wait_ge(spare_free, im.spare(("value", NT - 2)) + 1)
                    pe.wait_ge(odd_value_free, NT // 2 * (im.b + 1))
                else:
                    pe.wait_ge(ctx_lo, group)
                p = g // (NT // 2)
                n = GW if (g + 1) % (NT // 2) else GW - (TT - LAST)
                for k in range(NT):
                    for head in range(2):
                        f = (2 * p + head) * DK
                        last = pe.matmul(pv_ps[DK * head:DK * head + DK, 0:n], values[0:TT, k, f:f + DK],
                                         prob_t[:, head, k, 0:n], start=(k == 0), stop=(k == NT - 1),
                                         skip_group_check=True)
                last.then_inc(pv_full, 1)

            pe.wait_ge(ident_ok, 1)
            pe.wait_ge(wqk_kept, 16 * 4 * PAIRS)
            pro = Prologue()
            for work in PROLOGUE:
                if work[0] == "xt":
                    xt_tile(pro, work[1])
                else:
                    piece(pro, work[1], work[2])
            pe.wait_ge(cleared, 5)
            for u in range(AHEAD):
                scores(Image(0, first=True), u, pro)

            def body(im):
                for u in range(UNITS):
                    if not (im.last and u + AHEAD >= UNITS):
                        scores(im, u + AHEAD, im)
                    if u % PER_GROUP == 0 and u:
                        context(im, u // PER_GROUP - 1)
                    if u == 0 and not im.first:
                        context(Before(im), GROUPS - 1)
                    transposes(im, u)
                    for work in background(u, im.first, im.last):
                        if work[0] == "xt":
                            xt_tile(im, work[1])
                        elif work[0] == "piece":
                            piece(im, work[1], work[2])
                        elif work[0] == "value":
                            value_tile(im, work[1])
                        else:
                            out_tile(im.spare(work), im.b - 1, work[1])

            images(pe, body)
            end = Image(B - 1, last=True)
            context(end, GROUPS - 1)
            for t in range(NT):
                out_tile(end_spare(t), B - 1, t)

        @block.scalar
        def _(act):
            raw = [values[:, 0:KT, :], values[:, KT:2 * KT, :]]
            act.wait_ge(wqk_raw, 32)
            nc.scalar.activation(xt[:, 0, :, 0:D], raw[0], ACT.Copy, scale=-float(DK) ** -0.5).then_inc(w_hi, 1)
            nc.scalar.activation(ctx_t[:, 0, :, 0:D], raw[1], ACT.Copy).then_inc(w_hi, 1)
            act.wait_ge(wvo_raw, 32)
            nc.scalar.activation(wv_sb[:, 0, :, :], raw[0], ACT.Copy).then_inc(w_hi, 1)
            nc.scalar.activation(wo_sb[:, 0, :, :], raw[1], ACT.Copy).then_inc(w_hi, 1)

            def xt_hi(im, t):
                m = rows(t)
                act.wait_ge(spare_full, im.spare(("xt", t)) + 1)
                nc.scalar.activation(xt[:, 0, :, t * TT:t * TT + m],
                                     spare_ps[:, 0:KT * TT].rearrange("p (k t) -> p k t", k=KT)[:, :, 0:m],
                                     ACT.Copy).then_inc(spare_hi, 1)

            def piece_hi(im, p, j):
                kind, half = PIECES[j]
                cols = slice(half * HALF, half * HALF + HALF)
                act.wait_ge(spare_full, im.spare(("piece", p, j)) + 1)
                for head in range(2):
                    a = DK * head
                    dst = q_sb[a:a + DK, p % 2, head, cols] if kind == QUERY else k_sb[a:a + DK, p % 2, head, 0, cols]
                    bias = (bq_col if kind == QUERY else bk_col)[a:a + DK, p:p + 1]
                    nc.scalar.activation(dst, spare_ps[a:a + DK, 0:HALF], ACT.Identity, bias=bias
                                         ).then_inc(spare_hi, 1)

            def exponentials(im, u):
                unit = im.unit(u)
                act.wait_ge(scores_min, unit + 1)
                s = u % 4
                nc.scalar.activation(prob[:, u % BUFS, 0:S], prob[:, u % BUFS, 0:S], ACT.Exp, scale=-1.0,
                                     bias=row_min[:, s:s + 1], accum_out=row_sum[:, s:s + 1]).then_inc(exp_done, 1)

            def move_transposes(im, u):
                t, head = divmod(u % PER_PAIR, 2)
                unit = im.unit(u)
                c = t % 2 * TT
                for half, (full, moved) in enumerate(((t0_full, t0_moved), (t1_full, t1_moved))):
                    act.wait_ge(full, unit + 1)
                    group = GROUPS * im.b + u // PER_GROUP
                    if half == 0 and u % PER_GROUP == 0 and (not isinstance(group, int) or group):
                        act.wait_ge(pv_full, group)
                    nc.scalar.activation(prob_t[:, head, 4 * half:4 * half + 4, c:c + TT],
                                         t_ps[0:TT, half, 0:4 * TT].rearrange("p (k t) -> p k t", k=4),
                                         ACT.Copy).then_inc(moved, 1)

            def context_hi(im, g):
                p, c, n = group_columns(g)
                act.wait_ge(pv_full, GROUPS * im.b + g + 1)
                nc.scalar.activation(ctx_t[:, 0, p, c:c + n], pv_ps[:, 0:n], ACT.Copy).then_inc(ctx_hi, 1)

            act.wait_ge(wqk_kept, 16 * 4 * PAIRS)
            act.wait_ge(bq_scaled, 1)
            act.wait_ge(small_in, 16 * 6)
            pro = Prologue()
            for work in PROLOGUE:
                if work[0] == "xt":
                    xt_hi(pro, work[1])
                else:
                    piece_hi(pro, work[1], work[2])
            for u in range(AHEAD):
                exponentials(Image(0, first=True), u)

            def body(im):
                for u in range(UNITS):
                    if u % PER_GROUP == 0 and u:
                        context_hi(im, u // PER_GROUP - 1)
                    if u == 0 and not im.first:
                        context_hi(Before(im), GROUPS - 1)
                    move_transposes(im, u)
                    for work in background(u, im.first, im.last):
                        if work[0] == "xt":
                            xt_hi(im, work[1])
                    if not (im.last and u + AHEAD >= UNITS):
                        exponentials(im, u + AHEAD)
                    for work in background(u, im.first, im.last):
                        if work[0] == "piece":
                            piece_hi(im, work[1], work[2])

            images(act, body)
            context_hi(Image(B - 1, last=True), GROUPS - 1)

        @block.vector
        def _(dve):
            dve.wait_ge(line_in, 16)
            nc.vector.memset(grid[:, 0:2 * BIAS], 0.0).then_inc(grid_made, 1)
            pitch = grid.ap[0][0]
            centre = (GRID + 1) * BIAS + GRID - 1
            for n, (sh, sw) in enumerate(((1, 1), (1, -1), (-1, 1), (-1, -1))):
                quadrant = bass.AP(tensor=grid.tensor, offset=grid.offset + centre,
                                   ap=[[pitch, 1], [sh * BIAS, GRID], [sw, GRID]])
                by_distance = bass.AP(tensor=line_raw[:, :].tensor, offset=0, ap=[[BIAS, 1], [1, GRID], [1, GRID]])
                dve.wait_ge(grid_made, n + 1)
                nc.vector.tensor_scalar(quadrant, by_distance, -1.0, None, ALU.mult).then_inc(grid_made, 1)
            dve.wait_ge(small_in, 16 * 6)
            nc.vector.tensor_scalar(bq_col[:, :], bq_col[:, :], -float(DK) ** -0.5, None, ALU.mult
                                    ).then_inc(bq_scaled, 1)

            raw = [values[:, 0:KT, :], values[:, KT:2 * KT, :]]

            def weight_lo(n, dst, hi, src, scale):
                dve.wait_ge(w_hi, n)
                nc.vector.scalar_tensor_tensor(out=dst, in0=src, scalar=scale, in1=hi.bitcast(F32), op0=ALU.mult,
                                               op1=ALU.subtract).then_inc(w_lo, 1)

            weight_lo(1, xt[:, 1, :, 0:D], xt[:, 0, :, 0:D], raw[0], -float(DK) ** -0.5)
            weight_lo(2, ctx_t[:, 1, :, 0:D], ctx_t[:, 0, :, 0:D], raw[1], 1.0)
            nc.vector.memset(q_sb[:, :, :, S:SP_].bitcast(F32), 0.0).then_inc(cleared, 1)
            nc.vector.memset(prob[:, :, S:SP_], 0.0).then_inc(cleared, 1)
            nc.vector.memset(xt[:, :, :, S:SP_].bitcast(F32), 0.0).then_inc(cleared, 1)
            nc.vector.memset(ctx_t[:, :, :, S:SP_].bitcast(F32), 0.0).then_inc(cleared, 1)
            weight_lo(3, wv_sb[:, 1, :, :], wv_sb[:, 0, :, :], raw[0], 1.0)
            weight_lo(4, wo_sb[:, 1, :, :], wo_sb[:, 0, :, :], raw[1], 1.0)
            dve.wait_ge(w_lo, 4)
            nc.vector.memset(values[:, NT - 1, :], 0.0).then_inc(cleared, 1)

            def xt_lo(im, t):
                m = rows(t)
                dve.wait_ge(spare_hi, im.hi(("xt", t)) + 1)
                nc.vector.tensor_tensor(xt[:, 1, :, t * TT:t * TT + m],
                                        spare_ps[:, 0:KT * TT].rearrange("p (k t) -> p k t", k=KT)[:, :, 0:m],
                                        xt[:, 0, :, t * TT:t * TT + m].bitcast(F32), ALU.subtract
                                        ).then_inc(spare_free, 1)

            def piece_lo(im, p, j):
                kind, half = PIECES[j]
                cols = slice(half * HALF, half * HALF + HALF)
                for head in range(2):
                    a, c = DK * head, DK * (1 - head)
                    dve.wait_ge(spare_hi, im.hi(("piece", p, j)) + head + 1)
                    if kind == QUERY:
                        hi, lo = q_sb[a:a + DK, p % 2, head, cols], q_sb[c:c + DK, p % 2, head, cols]
                    else:
                        hi, lo = k_sb[a:a + DK, p % 2, head, 0, cols], k_sb[a:a + DK, p % 2, head, 1, cols]
                    bias = (bq_col if kind == QUERY else bk_col)[a:a + DK, p:p + 1]
                    nc.vector.scalar_tensor_tensor(out=lo, in0=spare_ps[a:a + DK, 0:HALF], scalar=bias,
                                                   in1=hi.bitcast(F32), op0=ALU.add, op1=ALU.subtract
                                                   ).then_inc(spare_free if head else spare_lo_a, 1)

            def value_move(im, t):
                if t % 2:
                    dve.wait_ge(odd_value_full, NT // 2 * im.b + t // 2 + 1)
                else:
                    dve.wait_ge(spare_full, im.spare(("value", t)) + 1)
                if t == 0 and im.first:
                    dve.wait_ge(cleared, 5)
                m = rows(t)
                nc.vector.tensor_tensor(values[0:m, t, :], (pv_ps if t % 2 else spare_ps)[0:m, :], bv_all[0:m, :],
                                        ALU.add).then_inc(odd_value_free if t % 2 else spare_free, 1)

            def biased_scores(im, u):
                unit = im.unit(u)
                t = u % PER_PAIR // 2
                dve.wait_ge(scores_full, unit + 1)
                if not isinstance(unit, int) or unit >= BUFS:
                    dve.wait_ge(t1_full, unit + 1 - BUFS)
                dve.nop(nofuse=True)
                w0 = WIN - GRID - ROWS * t
                nc.vector.tensor_tensor_reduce(
                    halves(prob[:, u % BUFS, 0:S]), s_ps[0:TT, u % 2, :, 0:HALF],
                    halves(window[:, w0:w0 + GRID, :].rearrange("p a c -> p (a c)")),
                    1.0, BIG, ALU.add, ALU.min, row_min[:, u % 4:u % 4 + 1]).then_inc(scores_min, 1)

            def normalise(im, u):
                unit = im.unit(u)
                s = u % 4
                dve.wait_ge(exp_done, unit + 1)
                nc.vector.reciprocal(row_inv[:, s:s + 1], row_sum[:, s:s + 1]).then_inc(inv_done, 1)
                dve.wait_ge(inv_done, unit + 1)
                nc.vector.tensor_scalar(prob[:, u % BUFS, 0:S], prob[:, u % BUFS, 0:S], row_inv[:, s:s + 1], None,
                                        ALU.mult).then_inc(prob_done, 1)

            def context_lo(im, g):
                p, c, n = group_columns(g)
                dve.wait_ge(ctx_hi, GROUPS * im.b + g + 1)
                nc.vector.tensor_tensor(ctx_t[:, 1, p, c:c + n], pv_ps[:, 0:n],
                                        ctx_t[:, 0, p, c:c + n].bitcast(F32), ALU.subtract).then_inc(ctx_lo, 1)

            def out_sum(use, b, t):
                i, m, n = t % 2, rows(t), NT * b + t + 1
                dve.wait_ge(spare_full, use + 1)
                dve.wait_ge(res_bias, n)
                nc.vector.tensor_tensor(y[0:m, i, :], spare_ps[0:m, :], y[0:m, i, :], ALU.add
                                        ).then_inc(spare_free, 1)
                dve.wait_ge(spare_free, use + 1)
                nc.vector.bn_stats(stats[0:m, i, :], y[0:m, i, :]).then_inc(stats_done, 1)
                dve.wait_ge(stats_done, n)
                dve.nop(nofuse=True)
                nc.vector.bn_aggr(mean_var[0:m, i, :], stats[0:m, i, :]).then_inc(mean_done, 1)

            def out_norm(b, t):
                i, m, n = t % 2, rows(t), NT * b + t + 1
                dve.wait_ge(rstd_done, n)
                nc.vector.tensor_scalar(y[0:m, i, :], y[0:m, i, :], mean_var[0:m, i, 0:1], rstd[0:m, i:i + 1],
                                        ALU.subtract, ALU.mult).then_inc(normed, 1)

            pro = Prologue()
            for work in PROLOGUE:
                if work[0] == "xt":
                    xt_lo(pro, work[1])
                else:
                    piece_lo(pro, work[1], work[2])
            dve.wait_ge(window_in, 16 * ROWS)
            dve.wait_ge(cleared, 5)
            biased_scores(Image(0, first=True), 0)
            for u in range(AHEAD - 1):
                biased_scores(Image(0, first=True), u + 1)
                normalise(Image(0, first=True), u)

            def body(im):
                for u in range(UNITS):
                    if u % PER_GROUP == 0 and u:
                        context_lo(im, u // PER_GROUP - 1)
                    if u == 0 and not im.first:
                        context_lo(Before(im), GROUPS - 1)
                    if not (im.last and u + AHEAD >= UNITS):
                        biased_scores(im, u + AHEAD)
                    if not (im.last and u + AHEAD > UNITS):
                        normalise(im, u + AHEAD - 1)
                    for work in background(u, im.first, im.last):
                        if work[0] == "xt":
                            xt_lo(im, work[1])
                        elif work[0] == "piece":
                            piece_lo(im, work[1], work[2])
                        elif work[0] == "value":
                            value_move(im, work[1])
                        else:
                            out_sum(im.spare(work), im.b - 1, work[1])
                    if not im.first and 2 <= u <= 2 * NT and u % 2 == 0:
                        out_norm(im.b - 1, u // 2 - 1)

            images(dve, body)
            context_lo(Image(B - 1, last=True), GROUPS - 1)
            for t in range(NT):
                out_sum(end_spare(t), B - 1, t)
                out_norm(B - 1, t)

        @block.gpsimd
        def _(pool):
            nc.gpsimd.memset(ident[:, :], 0.0).then_inc(ident_zero, 1)
            nc.gpsimd.memset(minus_half[:, :], -0.5).then_inc(ident_zero, 1)
            nc.gpsimd.memset(eps_col[:, :], EPS).then_inc(ident_zero, 1)
            pool.wait_ge(ident_zero, 3)
            nc.gpsimd.affine_select(out=ident[:, :], in_=ident[:, :], compare_op=ALU.not_equal, fill=1.0, base=0,
                                    pattern=[[-1, 128]], channel_multiplier=1).then_inc(ident_ok, 1)
            pool.wait_ge(small_in, 16 * 6)

            def add_bias(b, t):
                i, m = t % 2, rows(t)
                pool.wait_ge(res_in[i], 16 * (NT // 2 * b + t // 2 + 1))
                nc.gpsimd.tensor_tensor(y[0:m, i, :], y[0:m, i, :], bo_all[0:m, :], ALU.add).then_inc(res_bias, 1)

            def reciprocal_std(b, t):
                i, m, n = t % 2, rows(t), NT * b + t + 1
                pool.wait_ge(mean_done, n)
                nc.gpsimd.tensor_tensor(var_eps[0:m, i:i + 1], mean_var[0:m, i, 1:2], eps_col[0:m, :], ALU.add
                                        ).then_inc(eps_done, 1)
                pool.wait_ge(eps_done, n)
                nc.gpsimd.tensor_tensor(rstd[0:m, i:i + 1], var_eps[0:m, i:i + 1], minus_half[0:m, :], ALU.pow
                                        ).then_inc(rstd_done, 1)

            def scale_shift(b, t):
                i, m, n = t % 2, rows(t), NT * b + t + 1
                pool.wait_ge(normed, n)
                nc.gpsimd.tensor_tensor(y[0:m, i, :], y[0:m, i, :], gamma_all[0:m, :], ALU.mult
                                        ).then_inc(scaled, 1)
                pool.wait_ge(scaled, n)
                nc.gpsimd.tensor_tensor(y[0:m, i, :], y[0:m, i, :], beta_all[0:m, :], ALU.add
                                        ).then_inc(shifted, 1)

            def norm_image(b):
                add_bias(b, 0)
                for t in range(NT):
                    reciprocal_std(b, t)
                    if t == 0:
                        add_bias(b, 1)
                    scale_shift(b, t)
                    if t and t + 1 < NT:
                        add_bias(b, t + 1)

            with pool.Fori(0, B) as b:
                norm_image(b)


def group_columns(g):
    p, h = divmod(g, NT // 2)
    return p, h * GW, GW if h + 1 < NT // 2 else GW - (TT - LAST)


def end_spare(t):
    before = len([w for u in range(UNITS) for w in background(u, False, True)
                  if not (w[0] == "value" and w[1] % 2)])
    return Image(B - 1, last=True).spare0 + before + t


class Before:
    def __init__(self, im):
        self.b = im.b - 1


_INS = ["x", "L0_conv_wq", "L0_conv_bq", "L0_conv_wk", "L0_conv_bk", "L0_conv_wv", "L0_conv_bv", "L0_conv_wo",
        "L0_conv_bo", "L0_conv_ln_gamma", "L0_conv_ln_beta", "L0_conv_spatial_bias"]


def kernel(**inputs):
    import numpy as _np
    import concourse.bacc as _bacc
    from concourse import mybir as _mybir
    from concourse.bass_utils import run_bass_kernel_spmd as _run

    nc = _bacc.Bacc("TRN2", target_bir_lowering=False, num_devices=1)
    arrays, args = {}, []
    for name in _INS:
        a = _np.ascontiguousarray(inputs[name])
        arrays[f"in_{name}"] = a
        args.append(nc.dram_tensor(f"in_{name}", a.shape, _mybir.dt.from_np(a.dtype), kind="ExternalInput").ap())
    out = nc.dram_tensor("out", (B, GRID, GRID, D), _mybir.dt.float32, kind="ExternalOutput").ap()
    attention_layernorm(nc, *args, out)
    r = _run(nc, [arrays], core_ids=[0])
    return r.results[0]["out"]
```

```python
from contextlib import ExitStack

import concourse.bass as bass
from concourse import mybir

F32 = mybir.dt.float32
F32R = mybir.dt.float32r
ALU = mybir.AluOpType
ACT = mybir.ActivationFunctionType

B, GRID, D, HEADS = 16, 30, 512, 8
S = GRID * GRID
DK = D // HEADS
ROWS = 4
TT = ROWS * GRID
NT = -(-S // TT)
SP_ = NT * TT
LAST = S - (NT - 1) * TT
HALF = S // 2
KT = D // 128
PAIRS = HEADS // 2
UNITS = PAIRS * NT * 2
PER_PAIR = NT * 2
GROUPS = PAIRS * NT // 2
PER_GROUP = 4
GW = 2 * TT
BIAS = 2 * GRID - 1
WIN = 2 * NT * ROWS - ROWS - 2
EPS = 1e-5
BIG = 3.0e38
PARTS = 3
TERMS = [(0, 0), (0, 1), (1, 0)]
QUERY, KEY = 0, 1
AHEAD = 3
EXP_AHEAD = 2
NORM_AHEAD = 1
BUFS = 4
PIECES = [(KEY, 0), (KEY, 1), (QUERY, 0), (QUERY, 1)]


def piece_steps(p, plan):
    out, at = {}, 0
    for v, count in plan.items():
        out[v] = []
        while count:
            j, k = divmod(at, KT)
            n = min(count, KT - k)
            out[v].append(("steps", p, j, k, k + n))
            at, count = at + n, count - n
    assert at == KT * len(PIECES)
    return out


PLAN = [
    piece_steps(1, {6: 4, 7: 4, 10: 4, 11: 4}),
    piece_steps(2, {2: 2, 3: 2, 5: 2, 6: 2, 7: 2, 8: 2, 9: 2, 10: 2}),
    piece_steps(3, {2: 2, 3: 2, 5: 2, 6: 2, 7: 2, 8: 2, 9: 2, 10: 2}),
    piece_steps(0, {5: 2, 6: 2, 7: 2, 8: 2, 9: 2, 10: 2, 11: 4}),
]
XT_UNITS = list(range(3 * PER_PAIR - 4, 3 * PER_PAIR + 4))


def background(u, first, last):
    work = []
    p, v = divmod(u, PER_PAIR)
    if p == 0:
        if v < NT // 2:
            work += [("value", 2 * v), ("value", 2 * v + 1)]
        if v % PER_GROUP == 1 and not first:
            work += [("out", v // 2), ("out", v // 2 + 1)]
    if not (p == PAIRS - 1 and last):
        work += PLAN[p].get(v, [])
    if u in XT_UNITS and not last:
        work += [("xt", XT_UNITS.index(u))]
    return work


PROLOGUE = [("xt", t) for t in range(NT)] + [("steps", 0, j, 0, KT) for j in range(len(PIECES))]


def bank_of(use):
    if use[0] == "xt":
        return 0
    if use[0] == "piece":
        return (use[2] + (use[1] < 2)) % 2
    return use[1] % 2


def uses_of(works, bank=None):
    uses = []
    for w in works:
        if w[0] != "steps":
            uses.append(w)
        elif w[4] == KT:
            uses.append(("piece", w[1], w[2]))
    return [w for w in uses if bank is None or bank_of(w) == bank]


def works_of(units, first=False, last=False):
    return [w for u in units for w in background(u, first, last)]


def his_of(uses):
    return sum(2 if w[0] == "piece" else 1 if w[0] == "xt" else 0 for w in uses)


def counts(bank):
    lots = [uses_of(PROLOGUE, bank), uses_of(works_of(range(UNITS), first=True), bank),
            uses_of(works_of(range(UNITS)), bank)]
    return [len(x) for x in lots], [his_of(x) for x in lots]


COUNTS = [counts(0), counts(1)]


class Image:

    def __init__(self, b, first=False, last=False):
        self.b, self.first, self.last = b, first, last

    def start(self, bank, what):
        before, in_first, in_middle = COUNTS[bank][what]
        return before + (0 if self.first else (self.b - 1) * in_middle + in_first)

    def uses(self, bank):
        return uses_of(works_of(range(UNITS), self.first, self.last), bank)

    def use(self, use):
        bank = bank_of(use)
        return self.start(bank, 0) + self.uses(bank).index(use)

    def hi(self, use):
        bank = bank_of(use)
        uses = self.uses(bank)
        return self.start(bank, 1) + his_of(uses[:uses.index(use)])

    def uses_before_unit(self, u, bank):
        return self.start(bank, 0) + len(uses_of(works_of(range(u), self.first, self.last), bank))

    def unit(self, u):
        return self.b * UNITS + u


class Prologue:
    b, first, last = -1, True, False

    def use(self, use):
        return uses_of(PROLOGUE, bank_of(use)).index(use)

    def hi(self, use):
        uses = uses_of(PROLOGUE, bank_of(use))
        return his_of(uses[:uses.index(use)])


class End:

    def use(self, use):
        bank = bank_of(use)
        return Image(B - 1, last=True).uses_before_unit(UNITS, bank) + use[1] // 2


def images(eng, body):
    body(Image(0, first=True))
    with eng.Fori(1, B - 1) as b:
        body(Image(b))
    body(Image(B - 1, last=True))


def attention_layernorm(nc, x, wq, bq, wk, bk, wv, bv, wo, bo, gamma, beta, spatial_bias, out):
    x_t = x.rearrange("b h w d -> b (h w) d")
    out_t = out.rearrange("b h w d -> b (h w) d")

    with ExitStack() as ctx:
        def sb(name, shape, dt=F32):
            return ctx.enter_context(nc.sbuf_tensor(name, shape, dt))

        def sem(name):
            return ctx.enter_context(nc.semaphore(name))

        def dram(name, shape, dt):
            return nc.dram_tensor(name, shape, dt, kind="Internal").ap()

        wqk_split = dram("wqk_split", [PAIRS, 128, 2, 2, KT, 128], F32)
        bias_grid = dram("bias_grid", [BIAS + 2, BIAS], F32)
        bias_by_w = dram("bias_by_w", [GRID, BIAS + 2, GRID], F32)

        wqk_sb = sb("wqk_sb", [128, 2, KT, 128], F32R)
        wv_sb = sb("wv_sb", [128, 2, KT, D], F32R)
        wo_sb = sb("wo_sb", [128, 2, KT, D], F32R)
        window = sb("window", [TT, WIN, GRID])
        xt = sb("xt", [128, 2, KT, SP_], F32R)
        values = sb("values", [128, NT, D])
        q_sb = sb("q_sb", [128, 2, 2, SP_], F32R)
        k_sb = sb("k_sb", [128, 2, 2, 2, S], F32R)
        prob = sb("prob", [TT, BUFS, SP_])
        prob_t = sb("prob_t", [TT, 2, NT, GW])
        ctx_t = sb("ctx_t", [128, 2, PAIRS, SP_], F32R)
        tokens = sb("tokens", [TT, 2, D])
        x_nat = y = tokens
        bv_all = sb("bv_all", [TT, D])
        bo_all = sb("bo_all", [TT, D])
        gamma_all = sb("gamma_all", [TT, D])
        beta_all = sb("beta_all", [TT, D])
        bq_col = sb("bq_col", [128, PAIRS])
        bk_col = sb("bk_col", [128, PAIRS])
        ident = sb("ident", [128, 128])
        row_min = sb("row_min", [TT, 4])
        row_sum = sb("row_sum", [TT, 4])
        row_inv = sb("row_inv", [TT, 4])
        stats = sb("stats", [TT, 2, 6])
        mean_var = sb("mean_var", [TT, 2, 2])
        var_eps = sb("var_eps", [TT, 2])
        rstd = sb("rstd", [TT, 2])
        minus_half = sb("minus_half", [TT, 1])
        eps_col = sb("eps_col", [TT, 1])
        line_raw = sb("line_raw", [1, BIAS])
        grid = prob_t[0:1, :, :, :].rearrange("p h a b -> p (h a b)")[:, 0:(BIAS + 2) * BIAS]

        s_ps = ctx.enter_context(nc.psum_tensor("s_ps", [128, 2, 2, 512], F32))
        t_ps = ctx.enter_context(nc.psum_tensor("t_ps", [128, 2, 512], F32))
        pv_ps = ctx.enter_context(nc.psum_tensor("pv_ps", [128, 512], F32))
        spare_ps = ctx.enter_context(nc.psum_tensor("spare_ps", [128, 512], F32))

        wqk_raw = sem("wqk_raw")
        wvo_raw = sem("wvo_raw")
        w_hi = sem("w_hi")
        w_lo = sem("w_lo")
        wqk_kept = sem("wqk_kept")
        small_in = sem("small_in")
        bq_scaled = sem("bq_scaled")
        line_in = sem("line_in")
        grid_made = sem("grid_made")
        grid_kept = sem("grid_kept")
        by_w_kept = sem("by_w_kept")
        window_in = sem("window_in")
        cleared = sem("cleared")
        ident_zero = sem("ident_zero")
        ident_ok = sem("ident_ok")
        scores_full = sem("scores_full")
        scores_min = sem("scores_min")
        exp_done = sem("exp_done")
        inv_done = sem("inv_done")
        prob_done = sem("prob_done")
        t0_full = sem("t0_full")
        t1_full = sem("t1_full")
        t0_moved = sem("t0_moved")
        t1_moved = sem("t1_moved")
        pv_full = sem("pv_full")
        ctx_hi = sem("ctx_hi")
        ctx_lo = sem("ctx_lo")
        bank_full = [sem("spare_full"), sem("side_full")]
        bank_hi = [sem("spare_hi"), sem("side_hi")]
        bank_free = [sem("spare_free"), sem("side_free")]
        lo_a = sem("lo_a")
        x_in = [sem(f"x_in{i}") for i in range(2)]
        wqk_in = sem("wqk_in")
        k_copied = sem("k_copied")
        res_in = [sem(f"res_in{i}") for i in range(2)]
        res_bias = sem("res_bias")
        res_sum = sem("res_sum")
        stats_done = sem("stats_done")
        mean_done = sem("mean_done")
        eps_done = sem("eps_done")
        rstd_done = sem("rstd_done")
        normed = sem("normed")
        scaled = sem("scaled")
        shifted = sem("shifted")
        stored = [sem(f"stored{i}") for i in range(2)]

        block = ctx.enter_context(nc.Block())

        def rows(t):
            return LAST if t == NT - 1 else TT

        banks = [spare_ps, pv_ps]

        def halves(ap):
            return ap.rearrange("p (a c) -> p a c", a=2)

        @block.sync
        def _(sp):
            raw = [values[:, 0:KT, :], values[:, KT:2 * KT, :]]

            sp.dma_start(line_raw[:, :], spatial_bias[:, 0:1].rearrange("a b -> b a"),
                         allow_slow_non_contiguous=True).then_inc(line_in, 16)
            for r, w in zip(raw, (wq, wk)):
                sp.dma_start(r, w.rearrange("(t p) n -> p t n", p=128)).then_inc(wqk_raw, 16)
            sp.dma_start(bq_col[:, :], bq.rearrange("(t p) -> p t", p=128), allow_slow_non_contiguous=True).then_inc(small_in, 16)
            sp.dma_start(bk_col[:, :], bk.rearrange("(t p) -> p t", p=128), allow_slow_non_contiguous=True).then_inc(small_in, 16)
            for dst, src in ((bv_all, bv), (bo_all, bo), (gamma_all, gamma), (beta_all, beta)):
                sp.dma_start(dst[:, :], src.rearrange("(a d) -> a d", a=1).broadcast_to([TT, D])
                             ).then_inc(small_in, 16)

            def load_x(b, t):
                sp.dma_start(x_nat[0:rows(t), t % 2, :], x_t[b, t * TT:t * TT + rows(t), :]
                             ).then_inc(x_in[t % 2], 16)

            for t in range(2):
                load_x(0, t)

            sp.wait_ge(grid_made, 5)
            sp.dma_start(bias_grid, grid).then_inc(grid_kept, 16)
            sp.wait_ge(grid_kept, 16)
            for w in range(GRID):
                sp.dma_start(bias_by_w[w], bias_grid[:, GRID - 1 - w:2 * GRID - 1 - w]).then_inc(by_w_kept, 16)
            sp.wait_ge(by_w_kept, 16 * GRID)
            for hh in range(ROWS):
                r0 = ROWS - 1 - hh
                sp.dma_start(window[hh * GRID:(hh + 1) * GRID, :, :], bias_by_w[:, r0:r0 + WIN, :]
                             ).then_inc(window_in, 16)

            sp.wait_ge(w_lo, 2)
            for kind, src in ((QUERY, xt), (KEY, ctx_t)):
                for part in range(2):
                    for p in range(PAIRS):
                        sp.dma_start(wqk_split[p, :, kind, part, :, :],
                                     src[:, part, :, 128 * p:128 * p + 128].bitcast(F32)
                                     ).then_inc(wqk_kept, 16)
            for r, w in zip(raw, (wv, wo)):
                sp.dma_start(r, w.rearrange("(t p) n -> p t n", p=128)).then_inc(wvo_raw, 16)
            def copy_keys(im, p, j):
                use = ("piece", p, j)
                sp.wait_ge(bank_free[bank_of(use)], im.use(use) + 1)
                cols = slice(PIECES[j][1] * HALF, PIECES[j][1] * HALF + HALF)
                for head in range(2):
                    a, c = DK * head, DK * (1 - head)
                    sp.dma_start(k_sb[c:c + DK, p % 2, head, :, cols].bitcast(F32),
                                 k_sb[a:a + DK, p % 2, head, :, cols].bitcast(F32)
                                 ).then_inc(k_copied, 16)

            pro = Prologue()
            for t in range(2, NT):
                sp.wait_ge(bank_full[0], pro.use(("xt", t - 2)) + 1)
                load_x(0, t)
            for j, (kind, _) in enumerate(PIECES):
                if kind == KEY:
                    copy_keys(pro, 0, j)

            def load_residual(b, t):
                sp.dma_start(y[0:rows(t), t % 2, :], x_t[b, t * TT:t * TT + rows(t), :]
                             ).then_inc(res_in[t % 2], 16)

            def residuals(b, g):
                for t in (2 * g, 2 * g + 1):
                    load_residual(b, t)

            def store(b, g):
                for t in (2 * g, 2 * g + 1):
                    sp.wait_ge(shifted, NT * b + t + 1)
                    sp.dma_start(out_t[b, t * TT:t * TT + rows(t), :], tokens[0:rows(t), t % 2, :]
                                 ).then_inc(stored[t % 2], 16)
                if g + 1 < NT // 2:
                    for i in range(2):
                        sp.wait_ge(stored[i], 16 * (NT // 2 * b + g + 1))
                        load_residual(b, 2 * g + 2 + i)

            def body(im):
                for u in range(UNITS):
                    if u == 0 and not im.first:
                        residuals(im.b - 1, 0)
                    if not im.first and u % PER_GROUP == 3 and u < PER_PAIR:
                        store(im.b - 1, u // PER_GROUP)
                    for work in background(u - 1, im.first, im.last) if u else []:
                        if work[0] == "steps" and work[4] == KT and PIECES[work[2]][0] == KEY:
                            copy_keys(im, work[1], work[2])
                    if not im.last:
                        if u == XT_UNITS[0] - 8:
                            for t in range(2):
                                if im.first:
                                    sp.wait_ge(bank_full[0], COUNTS[0][0][0])
                                else:
                                    sp.wait_ge(stored[t], 16 * (NT // 2) * im.b)
                                    sp.nop(nofuse=True)
                                load_x(im.b + 1, t)
                        t = u - XT_UNITS[0] - 1
                        if 0 <= t < NT - 2:
                            sp.wait_ge(bank_full[0], im.use(("xt", t)) + 1)
                            load_x(im.b + 1, t + 2)
                        if t == NT - 1:
                            sp.wait_ge(bank_full[0], im.use(("xt", t)) + 1)
                            sp.nop(nofuse=True)

            images(sp, body)
            for i in range(2):
                sp.wait_ge(stored[i], 16 * (NT // 2) * (B - 1))
            residuals(B - 1, 0)
            for g in range(NT // 2):
                store(B - 1, g)
            for i in range(2):
                sp.wait_ge(stored[i], 16 * (NT // 2) * B)

        @block.tensor
        def _(pe):
            def xt_tile(im, t):
                n = im.use(("xt", t))
                if not isinstance(n, int) or n:
                    pe.wait_ge(bank_free[0], n)
                pe.wait_ge(x_in[t % 2], 16 * (NT // 2 * (im.b + 1) + t // 2 + 1))
                for k in range(KT):
                    last = pe.transpose(spare_ps[:, k * TT:k * TT + TT], x_nat[:, t % 2, 128 * k:128 * k + 128],
                                        ident[0:TT, 0:TT])
                last.then_inc(bank_full[0], 1)

            def bank_wait(im, u, use):
                bank, n = bank_of(use), im.use(use)
                if not isinstance(n, int) or n:
                    pe.wait_ge(bank_free[bank], n)
                if bank == 1 and u is not None and not (im.first and u < PER_GROUP):
                    pe.wait_ge(ctx_lo, GROUPS * im.b + u // PER_GROUP)

            def steps(im, u, p, j, k0, k1):
                kind, half = PIECES[j]
                bank = bank_of(("piece", p, j))
                if k0 == 0:
                    bank_wait(im, u, ("piece", p, j))
                    if half == 0:
                        pe.wait_ge(wqk_in, 32 * (PAIRS * (im.b + 1 if p == 0 else im.b) + p)
                                   + (16 if kind == KEY else 32))
                for k in range(k0, k1):
                    for i, (a, c) in enumerate(TERMS):
                        last = pe.matmul(banks[bank][:, 0:HALF], wqk_sb[:, a, k, :],
                                         xt[:, c, k, half * HALF:half * HALF + HALF],
                                         start=(k == 0 and i == 0), stop=(k == KT - 1 and i == PARTS - 1))
                if k1 == KT:
                    last.then_inc(bank_full[bank], 1)

            def value_tile(im, u, t):
                bank_wait(im, u, ("value", t))
                if t == 0 and im.first:
                    pe.wait_ge(w_lo, 4)
                for k in range(KT):
                    for i, (a, c) in enumerate(TERMS):
                        last = pe.matmul(banks[t % 2][0:TT, :], xt[:, a, k, t * TT:t * TT + TT], wv_sb[:, c, k, :],
                                         start=(k == 0 and i == 0), stop=(k == KT - 1 and i == PARTS - 1))
                last.then_inc(bank_full[t % 2], 1)

            def out_tile(im, u, b, t):
                bank_wait(im, u, ("out", t))
                if t == 0:
                    pe.wait_ge(ctx_lo, GROUPS * (b + 1))
                for k in range(PAIRS):
                    for i, (a, c) in enumerate(TERMS):
                        last = pe.matmul(banks[t % 2][0:TT, :], ctx_t[:, a, k, t * TT:t * TT + TT], wo_sb[:, c, k, :],
                                         start=(k == 0 and i == 0), stop=(k == PAIRS - 1 and i == PARTS - 1))
                last.then_inc(bank_full[t % 2], 1)

            def scores(im, u, pieces_of):
                p, v = divmod(u % UNITS, PER_PAIR)
                t, head = divmod(v, 2)
                unit = im.unit(u)
                if v == 0:
                    for j in (2, 3):
                        use = ("piece", p, j)
                        pe.wait_ge(bank_free[bank_of(use)], pieces_of.use(use) + 1)
                    pair = PAIRS * im.b + u // PER_PAIR
                    pe.wait_ge(k_copied, 64 * (pair + 1))
                if not isinstance(unit, int) or unit >= 2:
                    pe.wait_ge(scores_min, unit - 1)
                for half in range(2):
                    for part in range(2):
                        last = pe.matmul(s_ps[0:TT, u % 2, half, 0:HALF],
                                         q_sb[:, p % 2, head, t * TT:t * TT + TT],
                                         k_sb[:, p % 2, head, part, half * HALF:half * HALF + HALF],
                                         start=(part == 0), stop=(part == 1))
                last.then_inc(scores_full, 1)

            def transposes(im, u):
                unit = im.unit(u)
                pe.wait_ge(prob_done, unit + 1)
                for k in range(NT):
                    if k % 4 == 0 and (not isinstance(unit, int) or unit):
                        pe.wait_ge((t0_moved, t1_moved)[k // 4], unit)
                    last = pe.transpose(t_ps[0:TT, k // 4, k % 4 * TT:k % 4 * TT + TT],
                                        prob[:, u % BUFS, k * TT:k * TT + TT], ident[0:TT, 0:TT])
                    if k == 3:
                        last.then_inc(t0_full, 1)
                last.then_inc(t1_full, 1)

            def context(im, g, side_uses):
                group = GROUPS * im.b + g
                pe.wait_ge(t0_moved, PER_GROUP * (group + 1))
                pe.wait_ge(t1_moved, PER_GROUP * (group + 1))
                pe.wait_ge(bank_free[1], side_uses)
                if g == 0:
                    pe.wait_ge(bank_free[0], im.use(("value", NT - 2)) + 1)
                if not isinstance(group, int) or group:
                    pe.wait_ge(ctx_lo, group)
                p = g // (NT // 2)
                n = GW if (g + 1) % (NT // 2) else GW - (TT - LAST)
                for k in range(NT):
                    for head in range(2):
                        f = (2 * p + head) * DK
                        last = pe.matmul(pv_ps[DK * head:DK * head + DK, 0:n], values[0:TT, k, f:f + DK],
                                         prob_t[:, head, k, 0:n], start=(k == 0), stop=(k == NT - 1),
                                         skip_group_check=True)
                last.then_inc(pv_full, 1)

            pe.wait_ge(ident_ok, 1)
            pe.wait_ge(wqk_kept, 16 * 4 * PAIRS)
            pro = Prologue()
            for work in PROLOGUE:
                if work[0] == "xt":
                    xt_tile(pro, work[1])
                else:
                    steps(pro, None, *work[1:])
            pe.wait_ge(cleared, 5)
            for u in range(AHEAD):
                scores(Image(0, first=True), u, pro)

            def body(im):
                for u in range(UNITS):
                    if not (im.last and u + AHEAD >= UNITS):
                        scores(im, u + AHEAD, im)
                    if u % PER_GROUP == 0 and u:
                        context(im, u // PER_GROUP - 1, im.uses_before_unit(u, 1))
                    if u == 0 and not im.first:
                        context(Before(im), GROUPS - 1, im.uses_before_unit(0, 1))
                    transposes(im, u)
                    for work in background(u, im.first, im.last):
                        if work[0] == "xt":
                            xt_tile(im, work[1])
                        elif work[0] == "steps":
                            steps(im, u, *work[1:])
                        elif work[0] == "value":
                            value_tile(im, u, work[1])
                        else:
                            out_tile(im, u, im.b - 1, work[1])

            images(pe, body)
            end = Image(B - 1, last=True)
            context(end, GROUPS - 1, end.uses_before_unit(UNITS, 1))
            for t in range(NT):
                if t == 0:
                    pe.wait_ge(ctx_lo, GROUPS * B)
                out_tile(End(), None, B - 1, t)

        @block.scalar
        def _(act):
            raw = [values[:, 0:KT, :], values[:, KT:2 * KT, :]]
            act.wait_ge(wqk_raw, 32)
            nc.scalar.activation(xt[:, 0, :, 0:D], raw[0], ACT.Copy, scale=-float(DK) ** -0.5).then_inc(w_hi, 1)
            nc.scalar.activation(ctx_t[:, 0, :, 0:D], raw[1], ACT.Copy).then_inc(w_hi, 1)
            act.wait_ge(wvo_raw, 32)
            nc.scalar.activation(wv_sb[:, 0, :, :], raw[0], ACT.Copy).then_inc(w_hi, 1)
            nc.scalar.activation(wo_sb[:, 0, :, :], raw[1], ACT.Copy).then_inc(w_hi, 1)

            def xt_hi(im, t):
                m = rows(t)
                act.wait_ge(bank_full[0], im.use(("xt", t)) + 1)
                nc.scalar.activation(xt[:, 0, :, t * TT:t * TT + m],
                                     spare_ps[:, 0:KT * TT].rearrange("p (k t) -> p k t", k=KT)[:, :, 0:m],
                                     ACT.Copy).then_inc(bank_hi[0], 1)

            def piece_hi(im, p, j):
                kind, half = PIECES[j]
                cols = slice(half * HALF, half * HALF + HALF)
                bank = bank_of(("piece", p, j))
                act.wait_ge(bank_full[bank], im.use(("piece", p, j)) + 1)
                for head in range(2):
                    a = DK * head
                    dst = q_sb[a:a + DK, p % 2, head, cols] if kind == QUERY else k_sb[a:a + DK, p % 2, head, 0, cols]
                    bias = (bq_col if kind == QUERY else bk_col)[a:a + DK, p:p + 1]
                    nc.scalar.activation(dst, banks[bank][a:a + DK, 0:HALF], ACT.Identity, bias=bias
                                         ).then_inc(bank_hi[bank], 1)
                if half and not (im.last and p == PAIRS - 1 and kind == QUERY):
                    load_wqk(*((p, QUERY) if kind == KEY else ((p + 1) % PAIRS, KEY)))

            def exponentials(im, u):
                unit = im.unit(u)
                act.wait_ge(scores_min, unit + 1)
                s = u % 4
                nc.scalar.activation(prob[:, u % BUFS, 0:S], prob[:, u % BUFS, 0:S], ACT.Exp, scale=-1.0,
                                     bias=row_min[:, s:s + 1], accum_out=row_sum[:, s:s + 1]).then_inc(exp_done, 1)

            def move_transposes(im, u):
                t, head = divmod(u % PER_PAIR, 2)
                unit = im.unit(u)
                c, m = t % 2 * TT, rows(t)
                for half, (full, moved) in enumerate(((t0_full, t0_moved), (t1_full, t1_moved))):
                    act.wait_ge(full, unit + 1)
                    group = GROUPS * im.b + u // PER_GROUP
                    if half == 0 and u % PER_GROUP == 0 and (not isinstance(group, int) or group):
                        act.wait_ge(pv_full, group)
                    nc.scalar.activation(prob_t[:, head, 4 * half:4 * half + 4, c:c + m],
                                         t_ps[0:TT, half, 0:4 * TT].rearrange("p (k t) -> p k t", k=4)[:, :, 0:m],
                                         ACT.Copy).then_inc(moved, 1)

            def context_hi(im, g):
                p, c, n = group_columns(g)
                act.wait_ge(pv_full, GROUPS * im.b + g + 1)
                nc.scalar.activation(ctx_t[:, 0, p, c:c + n], pv_ps[:, 0:n], ACT.Copy).then_inc(ctx_hi, 1)

            def load_wqk(p, kind):
                act.dma_start(wqk_sb[:, :, :, :].bitcast(F32), wqk_split[p, :, kind]).then_inc(wqk_in, 16)

            act.wait_ge(wqk_kept, 16 * 4 * PAIRS)
            load_wqk(0, KEY)
            act.wait_ge(bq_scaled, 1)
            act.wait_ge(small_in, 16 * 6)
            pro = Prologue()
            for work in PROLOGUE:
                if work[0] == "xt":
                    xt_hi(pro, work[1])
                else:
                    piece_hi(pro, work[1], work[2])
            for u in range(EXP_AHEAD):
                exponentials(Image(0, first=True), u)

            def body(im):
                for u in range(UNITS):
                    if u % PER_GROUP == 0 and u:
                        context_hi(im, u // PER_GROUP - 1)
                    if u == 0 and not im.first:
                        context_hi(Before(im), GROUPS - 1)
                    move_transposes(im, u)
                    for work in background(u, im.first, im.last):
                        if work[0] == "xt":
                            xt_hi(im, work[1])
                    if not (im.last and u + EXP_AHEAD >= UNITS):
                        exponentials(im, u + EXP_AHEAD)
                    for work in background(u, im.first, im.last):
                        if work[0] == "steps" and work[4] == KT:
                            piece_hi(im, work[1], work[2])

            images(act, body)
            context_hi(Image(B - 1, last=True), GROUPS - 1)

        @block.vector
        def _(dve):
            dve.wait_ge(line_in, 16)
            nc.vector.memset(grid[:, 0:2 * BIAS], 0.0).then_inc(grid_made, 1)
            pitch = grid.ap[0][0]
            centre = (GRID + 1) * BIAS + GRID - 1
            for n, (sh, sw) in enumerate(((1, 1), (1, -1), (-1, 1), (-1, -1))):
                quadrant = bass.AP(tensor=grid.tensor, offset=grid.offset + centre,
                                   ap=[[pitch, 1], [sh * BIAS, GRID], [sw, GRID]])
                by_distance = bass.AP(tensor=line_raw[:, :].tensor, offset=0, ap=[[BIAS, 1], [1, GRID], [1, GRID]])
                dve.wait_ge(grid_made, n + 1)
                nc.vector.tensor_scalar(quadrant, by_distance, -1.0, None, ALU.mult).then_inc(grid_made, 1)
            dve.wait_ge(small_in, 16 * 6)
            nc.vector.tensor_scalar(bq_col[:, :], bq_col[:, :], -float(DK) ** -0.5, None, ALU.mult
                                    ).then_inc(bq_scaled, 1)

            raw = [values[:, 0:KT, :], values[:, KT:2 * KT, :]]

            def weight_lo(n, dst, hi, src, scale):
                dve.wait_ge(w_hi, n)
                nc.vector.scalar_tensor_tensor(out=dst, in0=src, scalar=scale, in1=hi.bitcast(F32), op0=ALU.mult,
                                               op1=ALU.subtract).then_inc(w_lo, 1)

            weight_lo(1, xt[:, 1, :, 0:D], xt[:, 0, :, 0:D], raw[0], -float(DK) ** -0.5)
            weight_lo(2, ctx_t[:, 1, :, 0:D], ctx_t[:, 0, :, 0:D], raw[1], 1.0)
            nc.vector.memset(q_sb[:, :, :, S:SP_].bitcast(F32), 0.0).then_inc(cleared, 1)
            nc.vector.memset(prob[:, :, S:SP_], 0.0).then_inc(cleared, 1)
            nc.vector.memset(xt[:, :, :, S:SP_].bitcast(F32), 0.0).then_inc(cleared, 1)
            nc.vector.memset(ctx_t[:, :, :, S:SP_].bitcast(F32), 0.0).then_inc(cleared, 1)
            weight_lo(3, wv_sb[:, 1, :, :], wv_sb[:, 0, :, :], raw[0], 1.0)
            weight_lo(4, wo_sb[:, 1, :, :], wo_sb[:, 0, :, :], raw[1], 1.0)
            dve.wait_ge(w_lo, 4)
            nc.vector.memset(values[:, NT - 1, :], 0.0).then_inc(cleared, 1)

            def xt_lo(im, t):
                m = rows(t)
                dve.wait_ge(bank_hi[0], im.hi(("xt", t)) + 1)
                nc.vector.tensor_tensor(xt[:, 1, :, t * TT:t * TT + m],
                                        spare_ps[:, 0:KT * TT].rearrange("p (k t) -> p k t", k=KT)[:, :, 0:m],
                                        xt[:, 0, :, t * TT:t * TT + m].bitcast(F32), ALU.subtract
                                        ).then_inc(bank_free[0], 1)

            def piece_lo(im, p, j):
                kind, half = PIECES[j]
                cols = slice(half * HALF, half * HALF + HALF)
                for head in range(2):
                    a, c = DK * head, DK * (1 - head)
                    bank = bank_of(("piece", p, j))
                    dve.wait_ge(bank_hi[bank], im.hi(("piece", p, j)) + head + 1)
                    if kind == QUERY:
                        hi, lo = q_sb[a:a + DK, p % 2, head, cols], q_sb[c:c + DK, p % 2, head, cols]
                    else:
                        hi, lo = k_sb[a:a + DK, p % 2, head, 0, cols], k_sb[a:a + DK, p % 2, head, 1, cols]
                    bias = (bq_col if kind == QUERY else bk_col)[a:a + DK, p:p + 1]
                    nc.vector.scalar_tensor_tensor(out=lo, in0=banks[bank][a:a + DK, 0:HALF], scalar=bias,
                                                   in1=hi.bitcast(F32), op0=ALU.add, op1=ALU.subtract
                                                   ).then_inc(bank_free[bank] if head else lo_a, 1)

            def value_move(im, t):
                dve.wait_ge(bank_full[t % 2], im.use(("value", t)) + 1)
                if t == 0 and im.first:
                    dve.wait_ge(cleared, 5)
                m = rows(t)
                nc.vector.tensor_tensor(values[0:m, t, :], banks[t % 2][0:m, :], bv_all[0:m, :],
                                        ALU.add).then_inc(bank_free[t % 2], 1)

            def biased_scores(im, u):
                unit = im.unit(u)
                t = u % PER_PAIR // 2
                dve.wait_ge(scores_full, unit + 1)
                if not isinstance(unit, int) or unit >= BUFS:
                    dve.wait_ge(t1_full, unit + 1 - BUFS)
                dve.nop(nofuse=True)
                w0 = WIN - GRID - ROWS * t
                nc.vector.tensor_tensor_reduce(
                    halves(prob[:, u % BUFS, 0:S]), s_ps[0:TT, u % 2, :, 0:HALF],
                    halves(window[:, w0:w0 + GRID, :].rearrange("p a c -> p (a c)")),
                    1.0, BIG, ALU.add, ALU.min, row_min[:, u % 4:u % 4 + 1]).then_inc(scores_min, 1)

            def invert_sum(im, u):
                s = u % 4
                dve.wait_ge(exp_done, im.unit(u) + 1)
                nc.vector.reciprocal(row_inv[:, s:s + 1], row_sum[:, s:s + 1]).then_inc(inv_done, 1)

            def normalise(im, u):
                s = u % 4
                dve.wait_ge(inv_done, im.unit(u) + 1)
                nc.vector.tensor_scalar(prob[:, u % BUFS, 0:S], prob[:, u % BUFS, 0:S], row_inv[:, s:s + 1], None,
                                        ALU.mult).then_inc(prob_done, 1)

            def context_lo(im, g):
                p, c, n = group_columns(g)
                dve.wait_ge(ctx_hi, GROUPS * im.b + g + 1)
                nc.vector.tensor_tensor(ctx_t[:, 1, p, c:c + n], pv_ps[:, 0:n],
                                        ctx_t[:, 0, p, c:c + n].bitcast(F32), ALU.subtract).then_inc(ctx_lo, 1)

            def out_sum(im, b, t):
                i, m, n = t % 2, rows(t), NT * b + t + 1
                use = im.use(("out", t))
                dve.wait_ge(bank_full[i], use + 1)
                dve.wait_ge(res_bias, n)
                nc.vector.tensor_tensor(y[0:m, i, :], banks[i][0:m, :], y[0:m, i, :], ALU.add
                                        ).then_inc(bank_free[i], 1)
                dve.wait_ge(bank_free[i], use + 1)
                nc.vector.bn_stats(stats[0:m, i, :], y[0:m, i, :]).then_inc(stats_done, 1)
                dve.wait_ge(stats_done, n)
                dve.nop(nofuse=True)
                nc.vector.bn_aggr(mean_var[0:m, i, :], stats[0:m, i, :]).then_inc(mean_done, 1)

            def out_norm(b, t):
                i, m, n = t % 2, rows(t), NT * b + t + 1
                dve.wait_ge(rstd_done, n)
                nc.vector.tensor_scalar(y[0:m, i, :], y[0:m, i, :], mean_var[0:m, i, 0:1], rstd[0:m, i:i + 1],
                                        ALU.subtract, ALU.mult).then_inc(normed, 1)

            pro = Prologue()
            for work in PROLOGUE:
                if work[0] == "xt":
                    xt_lo(pro, work[1])
                else:
                    piece_lo(pro, work[1], work[2])
            dve.wait_ge(window_in, 16 * ROWS)
            dve.wait_ge(cleared, 5)
            for u in range(AHEAD):
                biased_scores(Image(0, first=True), u)
            for u in range(NORM_AHEAD):
                invert_sum(Image(0, first=True), u)
                normalise(Image(0, first=True), u)

            def body(im):
                for u in range(UNITS):
                    if u % PER_GROUP == 0 and u:
                        context_lo(im, u // PER_GROUP - 1)
                    if u == 0 and not im.first:
                        context_lo(Before(im), GROUPS - 1)
                    if not (im.last and u + NORM_AHEAD >= UNITS):
                        invert_sum(im, u + NORM_AHEAD)
                    if not (im.last and u + NORM_AHEAD >= UNITS):
                        normalise(im, u + NORM_AHEAD)
                    if not (im.last and u + AHEAD >= UNITS):
                        biased_scores(im, u + AHEAD)
                    for work in background(u, im.first, im.last):
                        if work[0] == "xt":
                            xt_lo(im, work[1])
                        elif work[0] == "steps":
                            if work[4] == KT:
                                piece_lo(im, work[1], work[2])
                        elif work[0] == "value":
                            value_move(im, work[1])
                        else:
                            out_sum(im, im.b - 1, work[1])
                    if not im.first and u % PER_GROUP == 2 and u < PER_PAIR:
                        for t in (u // 2 - 1, u // 2):
                            out_norm(im.b - 1, t)

            images(dve, body)
            context_lo(Image(B - 1, last=True), GROUPS - 1)
            for g in range(NT // 2):
                for t in (2 * g, 2 * g + 1):
                    out_sum(End(), B - 1, t)
                for t in (2 * g, 2 * g + 1):
                    out_norm(B - 1, t)

        @block.gpsimd
        def _(pool):
            nc.gpsimd.memset(ident[:, :], 0.0).then_inc(ident_zero, 1)
            nc.gpsimd.memset(minus_half[:, :], -0.5).then_inc(ident_zero, 1)
            nc.gpsimd.memset(eps_col[:, :], EPS).then_inc(ident_zero, 1)
            pool.wait_ge(ident_zero, 3)
            nc.gpsimd.affine_select(out=ident[:, :], in_=ident[:, :], compare_op=ALU.not_equal, fill=1.0, base=0,
                                    pattern=[[-1, 128]], channel_multiplier=1).then_inc(ident_ok, 1)
            pool.wait_ge(small_in, 16 * 6)

            def add_bias(b, t):
                i, m = t % 2, rows(t)
                pool.wait_ge(res_in[i], 16 * (NT // 2 * b + t // 2 + 1))
                nc.gpsimd.tensor_tensor(y[0:m, i, :], y[0:m, i, :], bo_all[0:m, :], ALU.add).then_inc(res_bias, 1)

            def reciprocal_std(b, t):
                i, m, n = t % 2, rows(t), NT * b + t + 1
                pool.wait_ge(mean_done, n)
                nc.gpsimd.tensor_tensor(var_eps[0:m, i:i + 1], mean_var[0:m, i, 1:2], eps_col[0:m, :], ALU.add
                                        ).then_inc(eps_done, 1)
                pool.wait_ge(eps_done, n)
                nc.gpsimd.tensor_tensor(rstd[0:m, i:i + 1], var_eps[0:m, i:i + 1], minus_half[0:m, :], ALU.pow
                                        ).then_inc(rstd_done, 1)

            def scale_shift(b, t):
                i, m, n = t % 2, rows(t), NT * b + t + 1
                pool.wait_ge(normed, n)
                nc.gpsimd.tensor_tensor(y[0:m, i, :], y[0:m, i, :], gamma_all[0:m, :], ALU.mult
                                        ).then_inc(scaled, 1)
                pool.wait_ge(scaled, n)
                nc.gpsimd.tensor_tensor(y[0:m, i, :], y[0:m, i, :], beta_all[0:m, :], ALU.add
                                        ).then_inc(shifted, 1)

            def norm_image(b):
                for g in range(NT // 2):
                    tiles = (2 * g, 2 * g + 1)
                    for t in tiles:
                        add_bias(b, t)
                    for t in tiles:
                        reciprocal_std(b, t)
                    for t in tiles:
                        scale_shift(b, t)

            with pool.Fori(0, B) as b:
                norm_image(b)


def group_columns(g):
    p, h = divmod(g, NT // 2)
    return p, h * GW, GW if h + 1 < NT // 2 else GW - (TT - LAST)


class Before:
    def __init__(self, im):
        self.b = im.b - 1


_INS = ["x", "L0_conv_wq", "L0_conv_bq", "L0_conv_wk", "L0_conv_bk", "L0_conv_wv", "L0_conv_bv", "L0_conv_wo",
        "L0_conv_bo", "L0_conv_ln_gamma", "L0_conv_ln_beta", "L0_conv_spatial_bias"]


def kernel(**inputs):
    import numpy as _np
    import concourse.bacc as _bacc
    from concourse import mybir as _mybir
    from concourse.bass_utils import run_bass_kernel_spmd as _run

    nc = _bacc.Bacc("TRN2", target_bir_lowering=False, num_devices=1)
    arrays, args = {}, []
    for name in _INS:
        a = _np.ascontiguousarray(inputs[name])
        arrays[f"in_{name}"] = a
        args.append(nc.dram_tensor(f"in_{name}", a.shape, _mybir.dt.from_np(a.dtype), kind="ExternalInput").ap())
    out = nc.dram_tensor("out", (B, GRID, GRID, D), _mybir.dt.float32, kind="ExternalOutput").ap()
    attention_layernorm(nc, *args, out)
    r = _run(nc, [arrays], core_ids=[0])
    return r.results[0]["out"]
```

```python
from contextlib import ExitStack

import concourse.bass as bass
from concourse import mybir

F32 = mybir.dt.float32
F32R = mybir.dt.float32r
ALU = mybir.AluOpType
ACT = mybir.ActivationFunctionType

B, GRID, D, HEADS = 16, 30, 512, 8
S = GRID * GRID
DK = D // HEADS
ROWS = 4
TT = ROWS * GRID
NT = -(-S // TT)
SP_ = NT * TT
LAST = S - (NT - 1) * TT
HALF = S // 2
KT = D // 128
PAIRS = HEADS // 2
PER_PAIR = NT * 2 - 1
UNITS = PAIRS * PER_PAIR
GROUPS = PAIRS * NT // 2
PER_GROUP = 4
TAIL = PER_PAIR - 1
HEAD_ROWS = 64
TAIL_ROWS = HEAD_ROWS + LAST
GW = 2 * TT
BIAS = 2 * GRID - 1
WIN = 2 * (NT - 1) * ROWS - 2
EPS = 1e-5
BIG = 3.0e38
PARTS = 3
TERMS = [(0, 0), (0, 1), (1, 0)]
QUERY, KEY = 0, 1
AHEAD = 3
EXP_AHEAD = 2
NORM_AHEAD = 1
BUFS = 4
PIECES = [(KEY, 0), (KEY, 1), (QUERY, 0), (QUERY, 1)]


def piece_steps(p, plan):
    out, at = {}, 0
    for v, count in plan.items():
        out[v] = []
        while count:
            j, k = divmod(at, KT)
            n = min(count, KT - k)
            out[v].append(("steps", p, j, k, k + n))
            at, count = at + n, count - n
    assert at == KT * len(PIECES)
    return out


PLAN = [
    piece_steps(1, {3: 4, 6: 2, 7: 2, 8: 4, 10: 4}),
    piece_steps(2, {1: 2, 2: 1, 3: 1, 5: 2, 6: 1, 7: 1, 8: 3, 9: 3, 10: 2}),
    piece_steps(3, {1: 2, 2: 1, 3: 1, 5: 2, 6: 1, 7: 1, 8: 3, 9: 3, 10: 2}),
    piece_steps(0, {1: 2, 2: 2, 5: 2, 6: 1, 7: 1, 8: 3, 9: 3, 10: 2}),
]
PIECE_BANKS = [(1, 0, 1, 0), (0, 0, 1, 0), (0, 0, 1, 0), (0, 0, 1, 0)]
XT_UNITS = list(range(3 * PER_PAIR - 3, 3 * PER_PAIR + 5))


def group_of(u):
    return u // PER_PAIR * (NT // 2) + u % PER_PAIR // PER_GROUP


def ends_group(u):
    return u % PER_PAIR % PER_GROUP == 0


def units_of_groups(g):
    return g // (NT // 2) * PER_PAIR + g % (NT // 2) * PER_GROUP


def unit_rows(u):
    return TAIL_ROWS if u % PER_PAIR == TAIL else TT


def background(u, first, last):
    if u == UNITS:
        return [("final", NT - 2), ("final", NT - 1)] if last else []
    work = []
    p, v = divmod(u, PER_PAIR)
    if p == PAIRS - 1 and last and v > PER_GROUP and v % PER_GROUP in (1, 2):
        work += [("final", 2 * (v // PER_GROUP) - 2 + v % PER_GROUP - 1)]
    if p == 0:
        if v < NT // 2:
            work += [("value", 2 * v), ("value", 2 * v + 1)]
        if v % PER_GROUP == 1 and not first:
            work += [("out", v // 2), ("out", v // 2 + 1)]
    if not (p == PAIRS - 1 and last):
        work += PLAN[p].get(v, [])
    if u in XT_UNITS and not last:
        work += [("xt", XT_UNITS.index(u))]
    return work


PROLOGUE = [("first_xt", t) for t in range(NT)] + [("steps", 0, j, 0, KT) for j in range(len(PIECES))]


def bank_of(use):
    if use[0] == "xt":
        return 0
    if use[0] == "piece":
        return PIECE_BANKS[use[1]][use[2]]
    return use[1] % 2


def uses_of(works, bank=None):
    uses = []
    for w in works:
        if w[0] != "steps":
            uses.append(w)
        elif w[4] == KT:
            uses.append(("piece", w[1], w[2]))
    return [w for w in uses if bank is None or bank_of(w) == bank]


def works_of(units, first=False, last=False):
    return [w for u in units for w in background(u, first, last)]


def his_of(uses):
    return sum(2 if w[0] == "piece" else 1 if w[0] in ("xt", "first_xt") else 0 for w in uses)


def counts(bank):
    lots = [uses_of(PROLOGUE, bank), uses_of(works_of(range(UNITS), first=True), bank),
            uses_of(works_of(range(UNITS)), bank)]
    return [len(x) for x in lots], [his_of(x) for x in lots]


COUNTS = [counts(0), counts(1)]


class Image:
    xt = "xt"

    def __init__(self, b, first=False, last=False):
        self.b, self.first, self.last = b, first, last

    def start(self, bank, what):
        before, in_first, in_middle = COUNTS[bank][what]
        return before + (0 if self.first else (self.b - 1) * in_middle + in_first)

    def uses(self, bank):
        return uses_of(works_of(range(UNITS + 1), self.first, self.last), bank)

    def use(self, use):
        bank = bank_of(use)
        return self.start(bank, 0) + self.uses(bank).index(use)

    def hi(self, use):
        bank = bank_of(use)
        uses = self.uses(bank)
        return self.start(bank, 1) + his_of(uses[:uses.index(use)])

    def uses_before_unit(self, u, bank):
        return self.start(bank, 0) + len(uses_of(works_of(range(u), self.first, self.last), bank))

    def unit(self, u):
        return self.b * UNITS + u


class Prologue:
    b, first, last = -1, True, False
    xt = "first_xt"

    def use(self, use):
        return uses_of(PROLOGUE, bank_of(use)).index(use)

    def hi(self, use):
        uses = uses_of(PROLOGUE, bank_of(use))
        return his_of(uses[:uses.index(use)])


def images(eng, body):
    body(Image(0, first=True))
    with eng.Fori(1, B - 1) as b:
        body(Image(b))
    body(Image(B - 1, last=True))


def attention_layernorm(nc, x, wq, bq, wk, bk, wv, bv, wo, bo, gamma, beta, spatial_bias, out):
    x_t = x.rearrange("b h w d -> b (h w) d")
    out_t = out.rearrange("b h w d -> b (h w) d")

    with ExitStack() as ctx:
        def sb(name, shape, dt=F32):
            return ctx.enter_context(nc.sbuf_tensor(name, shape, dt))

        def sem(name):
            return ctx.enter_context(nc.semaphore(name))

        def dram(name, shape, dt):
            return nc.dram_tensor(name, shape, dt, kind="Internal").ap()

        wqk_split = dram("wqk_split", [PAIRS, 128, 2, 2, KT, 128], F32)
        bias_grid = dram("bias_grid", [BIAS + 2, BIAS], F32)
        bias_by_w = dram("bias_by_w", [GRID, BIAS + 2, GRID], F32)

        wqk_sb = sb("wqk_sb", [128, 2, KT, 128], F32R)
        wv_sb = sb("wv_sb", [128, 2, KT, D], F32R)
        wo_sb = sb("wo_sb", [128, 2, KT, D], F32R)
        window = sb("window", [TT, WIN, GRID])
        with nc.sbuf_tensor("last_tokens", [TT, NT, D], F32) as last_tokens:
            pass
        xt = sb("xt", [128, 2, KT, SP_], F32R)
        tail_window = sb("tail_window", [128, GRID, GRID])
        values = sb("values", [128, NT, D])
        q_sb = sb("q_sb", [128, 2, 2, SP_], F32R)
        k_sb = sb("k_sb", [128, 2, 2, 2, S], F32R)
        prob = sb("prob", [TAIL_ROWS, BUFS, SP_])
        prob_t = sb("prob_t", [TT, 2, NT, GW])
        ctx_t = sb("ctx_t", [128, 2, PAIRS, SP_], F32R)
        tokens = sb("tokens", [TT, 2, D])
        x_nat = y = tokens
        bv_all = sb("bv_all", [TT, D])
        bo_all = sb("bo_all", [TT, D])
        gamma_all = sb("gamma_all", [TT, D])
        beta_all = sb("beta_all", [TT, D])
        bq_col = sb("bq_col", [128, PAIRS])
        bk_col = sb("bk_col", [128, PAIRS])
        ident = sb("ident", [128, 128])
        row_min = sb("row_min", [TAIL_ROWS, 4])
        row_sum = sb("row_sum", [TAIL_ROWS, 4])
        row_inv = sb("row_inv", [TAIL_ROWS, 4])
        stats = sb("stats", [TT, 2, 6])
        mean_var = sb("mean_var", [TT, 2, 2])
        var_eps = sb("var_eps", [TT, 2])
        rstd = sb("rstd", [TT, 2])
        constants = sb("constants", [TT, 2])
        minus_half, eps_col = constants[:, 0:1], constants[:, 1:2]
        flat = prob_t[0:1, :, :, :].rearrange("p h a b -> p (h a b)")
        grid, line_raw = flat[:, 0:(BIAS + 2) * BIAS], flat[:, (BIAS + 2) * BIAS:(BIAS + 3) * BIAS]

        raw = [values[:, 0:KT, :], values[:, KT:2 * KT, :]]
        wk_split = k_sb[:, :, :, :, :].rearrange("p b h q s -> p (b h q s)")[:, 0:2 * KT * D].rearrange(
            "p (a k n) -> p a k n", a=2, k=KT)
        wq_split = ctx_t[:, :, :, 0:D]

        s_ps = ctx.enter_context(nc.psum_tensor("s_ps", [128, 2, 2, 512], F32))
        t_ps = ctx.enter_context(nc.psum_tensor("t_ps", [128, 2, 512], F32))
        pv_ps = ctx.enter_context(nc.psum_tensor("pv_ps", [128, 512], F32))
        spare_ps = ctx.enter_context(nc.psum_tensor("spare_ps", [128, 512], F32))

        wk_raw = sem("wk_raw")
        wq_raw = sem("wq_raw")
        wvo_raw = sem("wvo_raw")
        w_hi = sem("w_hi")
        w_lo = sem("w_lo")
        wk_kept = sem("wk_kept")
        wq_kept = sem("wq_kept")
        columns_in = sem("columns_in")
        small_in = sem("small_in")
        bq_scaled = sem("bq_scaled")
        line_in = sem("line_in")
        grid_made = sem("grid_made")
        grid_kept = sem("grid_kept")
        by_w_kept = sem("by_w_kept")
        window_in = sem("window_in")
        cleared = sem("cleared")
        ident_zero = sem("ident_zero")
        ident_ok = sem("ident_ok")
        scores_full = sem("scores_full")
        scores_min = sem("scores_min")
        exp_done = sem("exp_done")
        inv_done = sem("inv_done")
        prob_done = sem("prob_done")
        t0_full = sem("t0_full")
        t1_full = sem("t1_full")
        t0_moved = sem("t0_moved")
        t1_moved = sem("t1_moved")
        pv_full = sem("pv_full")
        ctx_hi = sem("ctx_hi")
        ctx_lo = sem("ctx_lo")
        bank_full = [sem("spare_full"), sem("side_full")]
        bank_hi = [sem("spare_hi"), sem("side_hi")]
        bank_free = [sem("spare_free"), sem("side_free")]
        lo_a = sem("lo_a")
        first_x_in = [sem(f"first_x_in{t}") for t in range(NT)]
        x_in = [sem(f"x_in{i}") for i in range(2)]
        wqk_in = sem("wqk_in")
        k_copied = sem("k_copied")
        res_in = [sem(f"res_in{i}") for i in range(2)]
        res_bias = sem("res_bias")
        stats_done = sem("stats_done")
        mean_done = sem("mean_done")
        eps_done = sem("eps_done")
        rstd_done = sem("rstd_done")
        normed = sem("normed")
        scaled = sem("scaled")
        shifted = sem("shifted")
        stored = [sem(f"stored{i}") for i in range(2)]

        block = ctx.enter_context(nc.Block())

        def rows(t):
            return LAST if t == NT - 1 else TT

        banks = [spare_ps, pv_ps]

        def halves(ap):
            return ap.rearrange("p (a c) -> p a c", a=2)

        def first_x(t):
            if t < 2:
                return x_nat[:, t, :]
            return prob[0:TT, :, :].rearrange("p b s -> p (b s)")[:, (t - 2) * D:(t - 1) * D]

        def copy_keys(eng, im, p, j):
            use = ("piece", p, j)
            eng.wait_ge(bank_free[bank_of(use)], im.use(use) + 1)
            cols = slice(PIECES[j][1] * HALF, PIECES[j][1] * HALF + HALF)
            for head in range(2):
                a, c = DK * head, DK * (1 - head)
                eng.dma_start(k_sb[c:c + DK, p % 2, head, :, cols].bitcast(F32),
                              k_sb[a:a + DK, p % 2, head, :, cols].bitcast(F32)).then_inc(k_copied, 16)

        def y_of(t, final):
            return last_tokens[0:rows(t), t, :] if final else y[0:rows(t), t % 2, :]

        @block.sync
        def _(sp):
            sp.dma_start(raw[0], wk.rearrange("(t p) n -> p t n", p=128)).then_inc(wk_raw, 16)
            sp.dma_start(line_raw[:, :], spatial_bias[:, 0:1].rearrange("a b -> b a"),
                         allow_slow_non_contiguous=True).then_inc(line_in, 16)
            for t in range(NT):
                sp.dma_start(first_x(t)[0:rows(t), :], x_t[0, t * TT:t * TT + rows(t), :]).then_inc(first_x_in[t], 16)
            sp.dma_start(raw[1], wq.rearrange("(t p) n -> p t n", p=128)).then_inc(wq_raw, 16)
            for dst, src in ((bk_col, bk), (bq_col, bq)):
                sp.dma_start(dst[:, :], src.rearrange("(t p) -> p t", p=128), allow_slow_non_contiguous=True
                             ).then_inc(columns_in, 16)
            sp.wait_ge(grid_made, 5)
            sp.dma_start(bias_grid, grid).then_inc(grid_kept, 16)

            for kind, src, kept, split in ((KEY, wk_split, wk_kept, 2), (QUERY, wq_split, wq_kept, 3)):
                sp.wait_ge(w_lo, split)
                for part in range(2):
                    for p in range(PAIRS):
                        sp.dma_start(wqk_split[p, :, kind, part, :, :],
                                     src[:, part, :, 128 * p:128 * p + 128].bitcast(F32)
                                     ).then_inc(kept, 16)
            for r, w in zip(raw, (wv, wo)):
                sp.dma_start(r, w.rearrange("(t p) n -> p t n", p=128)).then_inc(wvo_raw, 16)

            sp.wait_ge(grid_kept, 16)
            windows = bass.AP(tensor=bias_grid.tensor, offset=bias_grid.offset + GRID - 1,
                              ap=[[BIAS, BIAS + 2], [-1, GRID], [1, GRID]])
            sp.dma_start(bias_by_w.rearrange("w h v -> h w v"), windows, allow_slow_non_contiguous=True).then_inc(by_w_kept, 16)
            sp.wait_ge(by_w_kept, 16)
            for hh in range(ROWS):
                r0 = 2 * ROWS - 1 - hh
                sp.dma_start(window[hh * GRID:(hh + 1) * GRID, :, :], bias_by_w[:, r0:r0 + WIN, :]
                             ).then_inc(window_in, 16)
            sp.wait_ge(cleared, 1)
            for head in range(2):
                for hh in range(LAST // GRID):
                    row, r0 = HEAD_ROWS * head + GRID * hh, ROWS - 1 - hh
                    sp.dma_start(tail_window[row:row + GRID, :, :], bias_by_w[:, r0:r0 + GRID, :]
                                 ).then_inc(window_in, 16)
            for dst, src in ((bv_all, bv), (bo_all, bo), (gamma_all, gamma), (beta_all, beta)):
                sp.dma_start(dst[:, :], src.rearrange("(a d) -> a d", a=1).broadcast_to([TT, D])
                             ).then_inc(small_in, 16)

            def load_x(b, t):
                sp.dma_start(x_nat[0:rows(t), t % 2, :], x_t[b, t * TT:t * TT + rows(t), :]).then_inc(x_in[t % 2], 16)

            def load_residual(b, t):
                sp.dma_start(y[0:rows(t), t % 2, :], x_t[b, t * TT:t * TT + rows(t), :]
                             ).then_inc(res_in[t % 2], 16)

            def residuals(b, g):
                for t in (2 * g, 2 * g + 1):
                    load_residual(b, t)

            def store(b, g):
                for t in (2 * g, 2 * g + 1):
                    sp.wait_ge(shifted, NT * b + t + 1)
                    sp.dma_start(out_t[b, t * TT:t * TT + rows(t), :], tokens[0:rows(t), t % 2, :]
                                 ).then_inc(stored[t % 2], 16)
                if g + 1 < NT // 2:
                    for i in range(2):
                        sp.wait_ge(stored[i], 16 * (NT // 2 * b + g + 1))
                        load_residual(b, 2 * g + 2 + i)

            def store_final(t):
                sp.wait_ge(shifted, NT * (B - 1) + t + 1)
                sp.dma_start(out_t[B - 1, t * TT:t * TT + rows(t), :], y_of(t, True)).then_inc(stored[t % 2], 16)

            def body(im):
                for u in range(UNITS):
                    if im.last and u == (PAIRS - 1) * PER_PAIR:
                        use = ("piece", PAIRS - 1, len(PIECES) - 1)
                        sp.wait_ge(bank_full[bank_of(use)], im.use(use) + 1)
                        for t in range(NT):
                            sp.dma_start(y_of(t, True), x_t[B - 1, t * TT:t * TT + rows(t), :]
                                         ).then_inc(res_in[t % 2], 16)
                    for work in background(u - 3, im.first, im.last) if u > 3 else []:
                        if work[0] == "final":
                            store_final(work[1])
                    if u == 0 and not im.first:
                        residuals(im.b - 1, 0)
                    if not im.first and u % PER_GROUP == 3 and u <= PER_PAIR:
                        store(im.b - 1, u // PER_GROUP)
                    for work in background(u - 1, im.first, im.last) if u else []:
                        if work[0] == "steps" and work[4] == KT and PIECES[work[2]][0] == KEY:
                            copy_keys(sp, im, work[1], work[2])
                    if not im.last:
                        if u == XT_UNITS[0] - 8:
                            for t in range(2):
                                if im.first:
                                    sp.wait_ge(bank_full[t], COUNTS[t][0][0])
                                else:
                                    sp.wait_ge(stored[t], 16 * (NT // 2) * im.b)
                                    sp.nop(nofuse=True)
                                load_x(im.b + 1, t)
                        t = u - XT_UNITS[0] - 1
                        if 0 <= t < NT - 2:
                            sp.wait_ge(bank_full[0], im.use(("xt", t)) + 1)
                            load_x(im.b + 1, t + 2)
                        if t == NT - 1:
                            sp.wait_ge(bank_full[0], im.use(("xt", t)) + 1)
                            sp.nop(nofuse=True)

            images(sp, body)
            for u in range(UNITS - 3, UNITS + 1):
                for work in background(u, False, True):
                    if work[0] == "final":
                        store_final(work[1])
            for i in range(2):
                sp.wait_ge(stored[i], 16 * (NT // 2) * B)

        @block.tensor
        def _(pe):
            def xt_tile(im, t):
                bank, n = bank_of((im.xt, t)), im.use((im.xt, t))
                if not isinstance(n, int) or n:
                    pe.wait_ge(bank_free[bank], n)
                if isinstance(im, Prologue):
                    tile = first_x(t)
                    pe.wait_ge(first_x_in[t], 16)
                else:
                    tile = x_nat[:, t % 2, :]
                    pe.wait_ge(x_in[t % 2], 16 * (NT // 2 * im.b + t // 2 + 1))
                n_rows = rows(t) if isinstance(im, Prologue) else TT
                for k in range(KT):
                    last = pe.transpose(banks[bank][:, k * TT:k * TT + n_rows], tile[0:n_rows, 128 * k:128 * k + 128],
                                        ident[0:n_rows, 0:n_rows])
                last.then_inc(bank_full[bank], 1)

            def bank_wait(im, u, use):
                bank, n = bank_of(use), im.use(use)
                if not isinstance(n, int) or n:
                    pe.wait_ge(bank_free[bank], n)
                if bank == 1 and u is not None and not (im.first and u < PER_GROUP):
                    pe.wait_ge(ctx_lo, GROUPS * im.b + group_of(u))

            def steps(im, u, p, j, k0, k1):
                kind, half = PIECES[j]
                bank = bank_of(("piece", p, j))
                if k0 == 0:
                    bank_wait(im, u, ("piece", p, j))
                    if p == 0:
                        other = [(im.xt, t) for t in range(NT // 2 * (half + 1)) if bank_of((im.xt, t)) != bank]
                        for use in other[-1:]:
                            pe.wait_ge(bank_free[1 - bank], im.use(use) + 1)
                    if half == 0:
                        pe.wait_ge(wqk_in, 32 * (PAIRS * (im.b + 1 if p == 0 else im.b) + p)
                                   + (16 if kind == KEY else 32))
                for k in range(k0, k1):
                    for i, (a, c) in enumerate(TERMS):
                        last = pe.matmul(banks[bank][:, 0:HALF], wqk_sb[:, a, k, :],
                                         xt[:, c, k, half * HALF:half * HALF + HALF],
                                         start=(k == 0 and i == 0), stop=(k == KT - 1 and i == PARTS - 1))
                if k1 == KT:
                    last.then_inc(bank_full[bank], 1)

            def value_tile(im, u, t):
                bank_wait(im, u, ("value", t))
                if t == 0 and im.first:
                    pe.wait_ge(w_lo, 5)
                for k in range(KT):
                    for i, (a, c) in enumerate(TERMS):
                        last = pe.matmul(banks[t % 2][0:TT, :], xt[:, a, k, t * TT:t * TT + TT], wv_sb[:, c, k, :],
                                         start=(k == 0 and i == 0), stop=(k == KT - 1 and i == PARTS - 1))
                last.then_inc(bank_full[t % 2], 1)

            def out_tile(im, u, work):
                t = work[1]
                bank_wait(im, u, work)
                if work == ("out", 0):
                    pe.wait_ge(ctx_lo, GROUPS * im.b)
                if work[0] == "final" and t % 2 == 0:
                    pe.wait_ge(ctx_lo, GROUPS * (B - 1) + (PAIRS - 1) * NT // 2 + t // 2 + 1)
                for k in range(PAIRS):
                    for i, (a, c) in enumerate(TERMS):
                        last = pe.matmul(banks[t % 2][0:TT, :], ctx_t[:, a, k, t * TT:t * TT + TT], wo_sb[:, c, k, :],
                                         start=(k == 0 and i == 0), stop=(k == PAIRS - 1 and i == PARTS - 1))
                last.then_inc(bank_full[t % 2], 1)

            def scores(im, u, pieces_of):
                p, v = divmod(u % UNITS, PER_PAIR)
                t, head = divmod(v, 2)
                unit = im.unit(u)
                if v == 0:
                    for j in (2, 3):
                        use = ("piece", p, j)
                        pe.wait_ge(bank_free[bank_of(use)], pieces_of.use(use) + 1)
                    pair = PAIRS * im.b + u // PER_PAIR
                    pe.wait_ge(k_copied, 64 * (pair + 1))
                if not isinstance(unit, int) or unit >= 2:
                    pe.wait_ge(scores_min, unit - 1)
                blocks = [(head, t * TT, TT)] if v < TAIL else [(1, t * TT - HEAD_ROWS, TAIL_ROWS), (0, t * TT, HEAD_ROWS)]
                for half in range(2):
                    for head, q0, n in blocks:
                        for part in range(2):
                            last = pe.matmul(s_ps[0:n, u % 2, half, 0:HALF],
                                             q_sb[:, p % 2, head, q0:q0 + n],
                                             k_sb[:, p % 2, head, part, half * HALF:half * HALF + HALF],
                                             start=(part == 0), stop=(part == 1), skip_group_check=v == TAIL)
                last.then_inc(scores_full, 1)

            def transposes(im, u):
                unit = im.unit(u)
                pe.wait_ge(prob_done, unit + 1)
                n = unit_rows(u)
                for k in range(NT):
                    if k % 4 == 0 and (not isinstance(unit, int) or unit):
                        pe.wait_ge((t0_moved, t1_moved)[k // 4], unit)
                    last = pe.transpose(t_ps[0:TT, k // 4, k % 4 * 128:k % 4 * 128 + n],
                                        prob[0:n, u % BUFS, k * TT:k * TT + TT], ident[0:n, 0:n])
                    if k == 3:
                        last.then_inc(t0_full, 1)
                last.then_inc(t1_full, 1)

            def context(im, g, side_uses):
                group = GROUPS * im.b + g
                units = UNITS * im.b + units_of_groups(g + 1)
                pe.wait_ge(t0_moved, units)
                pe.wait_ge(t1_moved, units)
                pe.wait_ge(bank_free[1], side_uses)
                if g == 0:
                    pe.wait_ge(bank_free[0], im.use(("value", NT - 2)) + 1)
                if not isinstance(group, int) or group:
                    pe.wait_ge(ctx_lo, group)
                p = g // (NT // 2)
                n = GW if (g + 1) % (NT // 2) else GW - (TT - LAST)
                for k in range(NT):
                    for head in range(2):
                        f = (2 * p + head) * DK
                        last = pe.matmul(pv_ps[DK * head:DK * head + DK, 0:n], values[0:TT, k, f:f + DK],
                                         prob_t[:, head, k, 0:n], start=(k == 0), stop=(k == NT - 1),
                                         skip_group_check=True)
                last.then_inc(pv_full, 1)

            pe.wait_ge(ident_ok, 1)
            pro = Prologue()
            for work in PROLOGUE:
                if work[0] == "first_xt":
                    xt_tile(pro, work[1])
                else:
                    steps(pro, None, *work[1:])
            pe.wait_ge(cleared, 6)
            for u in range(AHEAD):
                scores(Image(0, first=True), u, pro)

            def body(im):
                for u in range(UNITS):
                    if not (im.last and u + AHEAD >= UNITS):
                        scores(im, u + AHEAD, im)
                    if ends_group(u) and u:
                        context(im, group_of(u) - 1, im.uses_before_unit(u, 1))
                    if u == 0 and not im.first:
                        context(Before(im), GROUPS - 1, im.uses_before_unit(0, 1))
                    transposes(im, u)
                    for work in background(u, im.first, im.last):
                        if work[0] == "xt":
                            xt_tile(im, work[1])
                        elif work[0] == "steps":
                            steps(im, u, *work[1:])
                        elif work[0] == "value":
                            value_tile(im, u, work[1])
                        else:
                            out_tile(im, u, work)

            images(pe, body)
            end = Image(B - 1, last=True)
            context(end, GROUPS - 1, end.uses_before_unit(UNITS, 1))
            for work in background(UNITS, False, True):
                out_tile(end, UNITS, work)

        @block.scalar
        def _(act):
            def weight_hi(dst, src, scale=1.0):
                nc.scalar.activation(dst, src, ACT.Copy, scale=scale).then_inc(w_hi, 1)

            act.wait_ge(wk_raw, 16)
            weight_hi(wqk_sb[:, 0, :, :], raw[0][:, :, 0:128])
            weight_hi(wk_split[:, 0], raw[0])
            act.wait_ge(wq_raw, 16)
            weight_hi(wq_split[:, 0], raw[1], -float(DK) ** -0.5)

            def xt_hi(im, t):
                m, bank = rows(t), bank_of((im.xt, t))
                act.wait_ge(bank_full[bank], im.use((im.xt, t)) + 1)
                nc.scalar.activation(xt[:, 0, :, t * TT:t * TT + m],
                                     banks[bank][:, 0:KT * TT].rearrange("p (k t) -> p k t", k=KT)[:, :, 0:m],
                                     ACT.Copy).then_inc(bank_hi[bank], 1)

            def piece_hi(im, p, j):
                kind, half = PIECES[j]
                cols = slice(half * HALF, half * HALF + HALF)
                bank = bank_of(("piece", p, j))
                act.wait_ge(bank_full[bank], im.use(("piece", p, j)) + 1)
                for head in range(2):
                    a = DK * head
                    dst = q_sb[a:a + DK, p % 2, head, cols] if kind == QUERY else k_sb[a:a + DK, p % 2, head, 0, cols]
                    bias = (bq_col if kind == QUERY else bk_col)[a:a + DK, p:p + 1]
                    nc.scalar.activation(dst, banks[bank][a:a + DK, 0:HALF], ACT.Identity, bias=bias
                                         ).then_inc(bank_hi[bank], 1)
                if half and not (im.last and p == PAIRS - 1 and kind == QUERY):
                    load_wqk(im, *((p, QUERY) if kind == KEY else ((p + 1) % PAIRS, KEY)))

            def exponentials(im, u):
                unit = im.unit(u)
                act.wait_ge(scores_min, unit + 1)
                s, n = u % 4, unit_rows(u)
                nc.scalar.activation(prob[0:n, u % BUFS, 0:S], prob[0:n, u % BUFS, 0:S], ACT.Exp, scale=-1.0,
                                     bias=row_min[0:n, s:s + 1], accum_out=row_sum[0:n, s:s + 1]).then_inc(exp_done, 1)

            def move_transposes(im, u):
                t, head = divmod(u % PER_PAIR, 2)
                unit = im.unit(u)
                c = t % 2 * TT
                for half, (full, moved) in enumerate(((t0_full, t0_moved), (t1_full, t1_moved))):
                    act.wait_ge(full, unit + 1)
                    group = GROUPS * im.b + group_of(u)
                    if half == 0 and ends_group(u) and (not isinstance(group, int) or group):
                        act.wait_ge(pv_full, group)
                    if t < NT - 1:
                        dst = prob_t[:, head, 4 * half:4 * half + 4, c:c + TT]
                        src = t_ps[0:TT, half, :].rearrange("p (k t) -> p k t", k=4)[:, :, 0:TT]
                    else:
                        dst = prob_t[:, :, 4 * half:4 * half + 4, c:c + LAST]
                        src = t_ps[0:TT, half, :].rearrange("p (k h t) -> p h k t", k=4, h=2)[:, :, :, 0:LAST]
                    nc.scalar.activation(dst, src, ACT.Copy).then_inc(moved, 1)

            def context_hi(im, g):
                p, c, n = group_columns(g)
                act.wait_ge(pv_full, GROUPS * im.b + g + 1)
                nc.scalar.activation(ctx_t[:, 0, p, c:c + n], pv_ps[:, 0:n], ACT.Copy).then_inc(ctx_hi, 1)

            def load_wqk(im, p, kind):
                split = wqk_split[p, :, kind]
                if isinstance(im, Prologue) and kind == QUERY:
                    split = wq_split[:, :, :, 0:128].bitcast(F32)
                act.dma_start(wqk_sb[:, :, :, :].bitcast(F32), split).then_inc(wqk_in, 16)

            pro = Prologue()
            for t in range(NT):
                xt_hi(pro, t)
            act.wait_ge(wk_kept, 16 * 2 * PAIRS)
            act.wait_ge(columns_in, 32)
            piece_hi(pro, 0, 0)
            piece_hi(pro, 0, 1)
            for j in range(2):
                copy_keys(act, pro, 0, j)
            act.wait_ge(wvo_raw, 32)
            weight_hi(wv_sb[:, 0, :, :], raw[0])
            weight_hi(wo_sb[:, 0, :, :], raw[1])
            act.wait_ge(bq_scaled, 1)
            for j in range(2, 4):
                act.wait_ge(wq_kept, 16 * 2 * PAIRS)
                piece_hi(pro, 0, j)
            for u in range(EXP_AHEAD):
                exponentials(Image(0, first=True), u)

            def body(im):
                for u in range(UNITS):
                    if ends_group(u) and u:
                        context_hi(im, group_of(u) - 1)
                    if u == 0 and not im.first:
                        context_hi(Before(im), GROUPS - 1)
                    move_transposes(im, u)
                    for work in background(u, im.first, im.last):
                        if work[0] == "xt":
                            xt_hi(im, work[1])
                    if not (im.last and u + EXP_AHEAD >= UNITS):
                        exponentials(im, u + EXP_AHEAD)
                    for work in background(u, im.first, im.last):
                        if work[0] == "steps" and work[4] == KT:
                            piece_hi(im, work[1], work[2])

            images(act, body)
            context_hi(Image(B - 1, last=True), GROUPS - 1)

        @block.vector
        def _(dve):
            dve.wait_ge(line_in, 16)
            nc.vector.memset(grid[:, 0:2 * BIAS], 0.0).then_inc(grid_made, 1)
            pitch = grid.ap[0][0]
            centre = (GRID + 1) * BIAS + GRID - 1
            for n, (sh, sw) in enumerate(((1, 1), (1, -1), (-1, 1), (-1, -1))):
                quadrant = bass.AP(tensor=grid.tensor, offset=grid.offset + centre,
                                   ap=[[pitch, 1], [sh * BIAS, GRID], [sw, GRID]])
                by_distance = bass.AP(tensor=line_raw.tensor, offset=line_raw.offset, ap=[[pitch, 1], [1, GRID], [1, GRID]])
                dve.wait_ge(grid_made, n + 1)
                nc.vector.tensor_scalar(quadrant, by_distance, -1.0, None, ALU.mult).then_inc(grid_made, 1)
            def weight_lo(n, dst, hi, src, scale):
                dve.wait_ge(w_hi, n)
                nc.vector.scalar_tensor_tensor(out=dst, in0=src, scalar=scale, in1=hi.bitcast(F32), op0=ALU.mult,
                                               op1=ALU.subtract).then_inc(w_lo, 1)

            nc.vector.memset(tail_window[:, :, :], 0.0).then_inc(cleared, 1)
            nc.vector.memset(q_sb[:, :, :, S:SP_].bitcast(F32), 0.0).then_inc(cleared, 1)
            nc.vector.memset(xt[:, :, :, S:SP_].bitcast(F32), 0.0).then_inc(cleared, 1)
            nc.vector.memset(ctx_t[:, :, :, S:SP_].bitcast(F32), 0.0).then_inc(cleared, 1)
            weight_lo(1, wqk_sb[:, 1, :, :], wqk_sb[:, 0, :, :], raw[0][:, :, 0:128], 1.0)
            dve.wait_ge(w_lo, 1)
            dve.nop(nofuse=True).then_inc(wqk_in, 16)
            weight_lo(2, wk_split[:, 1], wk_split[:, 0], raw[0], 1.0)
            weight_lo(3, wq_split[:, 1], wq_split[:, 0], raw[1], -float(DK) ** -0.5)
            dve.wait_ge(columns_in, 32)
            nc.vector.tensor_scalar(bq_col[:, :], bq_col[:, :], -float(DK) ** -0.5, None, ALU.mult
                                    ).then_inc(bq_scaled, 1)

            def xt_lo(im, t):
                m, bank = rows(t), bank_of((im.xt, t))
                dve.wait_ge(bank_hi[bank], im.hi((im.xt, t)) + 1)
                nc.vector.tensor_tensor(xt[:, 1, :, t * TT:t * TT + m],
                                        banks[bank][:, 0:KT * TT].rearrange("p (k t) -> p k t", k=KT)[:, :, 0:m],
                                        xt[:, 0, :, t * TT:t * TT + m].bitcast(F32), ALU.subtract
                                        ).then_inc(bank_free[bank], 1)

            def piece_lo(im, p, j):
                kind, half = PIECES[j]
                cols = slice(half * HALF, half * HALF + HALF)
                for head in range(2):
                    a, c = DK * head, DK * (1 - head)
                    bank = bank_of(("piece", p, j))
                    dve.wait_ge(bank_hi[bank], im.hi(("piece", p, j)) + head + 1)
                    if kind == QUERY:
                        hi, lo = q_sb[a:a + DK, p % 2, head, cols], q_sb[c:c + DK, p % 2, head, cols]
                    else:
                        hi, lo = k_sb[a:a + DK, p % 2, head, 0, cols], k_sb[a:a + DK, p % 2, head, 1, cols]
                    bias = (bq_col if kind == QUERY else bk_col)[a:a + DK, p:p + 1]
                    nc.vector.scalar_tensor_tensor(out=lo, in0=banks[bank][a:a + DK, 0:HALF], scalar=bias,
                                                   in1=hi.bitcast(F32), op0=ALU.add, op1=ALU.subtract
                                                   ).then_inc(bank_free[bank] if head else lo_a, 1)

            def value_move(im, t):
                dve.wait_ge(bank_full[t % 2], im.use(("value", t)) + 1)
                if t == 0 and im.first:
                    dve.wait_ge(cleared, 6)
                m = rows(t)
                nc.vector.tensor_tensor(values[0:m, t, :], banks[t % 2][0:m, :], bv_all[0:m, :],
                                        ALU.add).then_inc(bank_free[t % 2], 1)

            def biased_scores(im, u):
                unit = im.unit(u)
                t = u % PER_PAIR // 2
                dve.wait_ge(scores_full, unit + 1)
                if not isinstance(unit, int) or unit >= BUFS:
                    dve.wait_ge(t1_full, unit + 1 - BUFS)
                dve.nop(nofuse=True)
                n, w0 = unit_rows(u), WIN - GRID - ROWS * t
                bias = window[:, w0:w0 + GRID, :] if t < NT - 1 else tail_window[0:n, :, :]
                nc.vector.tensor_tensor_reduce(
                    halves(prob[0:n, u % BUFS, 0:S]), s_ps[0:n, u % 2, :, 0:HALF],
                    halves(bias.rearrange("p a c -> p (a c)")),
                    1.0, BIG, ALU.add, ALU.min, row_min[0:n, u % 4:u % 4 + 1]).then_inc(scores_min, 1)

            def invert_sum(im, u):
                s, n = u % 4, unit_rows(u)
                dve.wait_ge(exp_done, im.unit(u) + 1)
                nc.vector.reciprocal(row_inv[0:n, s:s + 1], row_sum[0:n, s:s + 1]).then_inc(inv_done, 1)

            def normalise(im, u):
                s, n = u % 4, unit_rows(u)
                dve.wait_ge(inv_done, im.unit(u) + 1)
                nc.vector.tensor_scalar(prob[0:n, u % BUFS, 0:S], prob[0:n, u % BUFS, 0:S], row_inv[0:n, s:s + 1], None,
                                        ALU.mult).then_inc(prob_done, 1)

            def context_lo(im, g):
                p, c, n = group_columns(g)
                dve.wait_ge(ctx_hi, GROUPS * im.b + g + 1)
                nc.vector.tensor_tensor(ctx_t[:, 1, p, c:c + n], pv_ps[:, 0:n],
                                        ctx_t[:, 0, p, c:c + n].bitcast(F32), ALU.subtract).then_inc(ctx_lo, 1)

            def out_sum(im, work):
                t, final = work[1], work[0] == "final"
                y = y_of(t, final)
                i, m, n = t % 2, rows(t), NT * (im.b if final else im.b - 1) + t + 1
                use = im.use(work)
                dve.wait_ge(bank_full[i], use + 1)
                dve.wait_ge(res_bias, n)
                nc.vector.tensor_tensor(y, banks[i][0:m, :], y, ALU.add).then_inc(bank_free[i], 1)
                dve.wait_ge(bank_free[i], use + 1)
                nc.vector.bn_stats(stats[0:m, i, :], y).then_inc(stats_done, 1)
                dve.wait_ge(stats_done, n)
                dve.nop(nofuse=True)
                nc.vector.bn_aggr(mean_var[0:m, i, :], stats[0:m, i, :]).then_inc(mean_done, 1)

            def out_norm(b, t, final=False):
                i, m, n = t % 2, rows(t), NT * b + t + 1
                y = y_of(t, final)
                dve.wait_ge(rstd_done, n)
                nc.vector.tensor_scalar(y, y, mean_var[0:m, i, 0:1], rstd[0:m, i:i + 1],
                                        ALU.subtract, ALU.mult).then_inc(normed, 1)

            pro = Prologue()
            for t in range(NT):
                xt_lo(pro, t)
            nc.vector.memset(prob[:, :, S:SP_], 0.0).then_inc(cleared, 1)
            for j in range(2):
                piece_lo(pro, 0, j)
            weight_lo(4, wv_sb[:, 1, :, :], wv_sb[:, 0, :, :], raw[0], 1.0)
            weight_lo(5, wo_sb[:, 1, :, :], wo_sb[:, 0, :, :], raw[1], 1.0)
            dve.wait_ge(w_lo, 5)
            nc.vector.memset(values[:, NT - 1, :], 0.0).then_inc(cleared, 1)
            dve.wait_ge(small_in, 16 * 4)
            for j in range(2, 4):
                piece_lo(pro, 0, j)
            dve.wait_ge(window_in, 16 * (ROWS + 2 * LAST // GRID))
            dve.wait_ge(cleared, 6)
            for u in range(AHEAD):
                biased_scores(Image(0, first=True), u)
            for u in range(NORM_AHEAD):
                invert_sum(Image(0, first=True), u)
                normalise(Image(0, first=True), u)

            def body(im):
                for u in range(UNITS):
                    if not (im.last and u + NORM_AHEAD >= UNITS):
                        invert_sum(im, u + NORM_AHEAD)
                    if not (im.last and u + NORM_AHEAD >= UNITS):
                        normalise(im, u + NORM_AHEAD)
                    if ends_group(u) and u:
                        context_lo(im, group_of(u) - 1)
                    if u == 0 and not im.first:
                        context_lo(Before(im), GROUPS - 1)
                    if not (im.last and u + AHEAD >= UNITS):
                        biased_scores(im, u + AHEAD)
                    works = background(u, im.first, im.last)
                    for work in works:
                        if work[0] == "xt":
                            xt_lo(im, work[1])
                    for work in works:
                        if work[0] == "steps" and work[4] == KT:
                            piece_lo(im, work[1], work[2])
                        elif work[0] == "value":
                            value_move(im, work[1])
                        elif work[0] in ("out", "final"):
                            out_sum(im, work)
                    for work in background(u - 1, im.first, im.last) if u else []:
                        if work[0] == "final":
                            out_norm(B - 1, work[1], final=True)
                    if not im.first and u % PER_GROUP == 2 and u < PER_PAIR:
                        for t in (u // 2 - 1, u // 2):
                            out_norm(im.b - 1, t)

            images(dve, body)
            context_lo(Image(B - 1, last=True), GROUPS - 1)
            for work in background(UNITS - 1, False, True):
                if work[0] == "final":
                    out_norm(B - 1, work[1], final=True)
            for work in background(UNITS, False, True):
                out_sum(Image(B - 1, last=True), work)
            for work in background(UNITS, False, True):
                out_norm(B - 1, work[1], final=True)

        @block.gpsimd
        def _(pool):
            nc.gpsimd.memset(ident[:, :], 0.0).then_inc(ident_zero, 1)
            nc.gpsimd.memset(minus_half, -0.5).then_inc(ident_zero, 1)
            nc.gpsimd.memset(eps_col, EPS).then_inc(ident_zero, 1)
            pool.wait_ge(ident_zero, 3)
            nc.gpsimd.affine_select(out=ident[:, :], in_=ident[:, :], compare_op=ALU.not_equal, fill=1.0, base=0,
                                    pattern=[[-1, 128]], channel_multiplier=1).then_inc(ident_ok, 1)
            pool.wait_ge(small_in, 16 * 4)

            def add_bias(t, final=False):
                y = y_of(t, final)
                nc.gpsimd.tensor_tensor(y, y, bo_all[0:rows(t), :], ALU.add).then_inc(res_bias, 1)

            def reciprocal_std(b, t):
                i, m, n = t % 2, rows(t), NT * b + t + 1
                pool.wait_ge(mean_done, n)
                nc.gpsimd.tensor_tensor(var_eps[0:m, i:i + 1], mean_var[0:m, i, 1:2], eps_col[0:m, :], ALU.add
                                        ).then_inc(eps_done, 1)
                pool.wait_ge(eps_done, n)
                nc.gpsimd.tensor_tensor(rstd[0:m, i:i + 1], var_eps[0:m, i:i + 1], minus_half[0:m, :], ALU.pow
                                        ).then_inc(rstd_done, 1)

            def scale_shift(b, t, final=False):
                m, n, y = rows(t), NT * b + t + 1, y_of(t, final)
                pool.wait_ge(normed, n)
                nc.gpsimd.tensor_tensor(y, y, gamma_all[0:m, :], ALU.mult).then_inc(scaled, 1)
                pool.wait_ge(scaled, n)
                nc.gpsimd.tensor_tensor(y, y, beta_all[0:m, :], ALU.add).then_inc(shifted, 1)

            with pool.Fori(0, B - 1) as b:
                for g in range(NT // 2):
                    tiles = (2 * g, 2 * g + 1)
                    for t in tiles:
                        pool.wait_ge(res_in[t % 2], 16 * (NT // 2 * b + g + 1))
                        add_bias(t)
                    for t in tiles:
                        reciprocal_std(b, t)
                    for t in tiles:
                        scale_shift(b, t)
            for i in range(2):
                pool.wait_ge(res_in[i], 16 * (NT // 2) * B)
            for t in range(NT):
                add_bias(t, final=True)
            for g in range(NT // 2):
                for t in (2 * g, 2 * g + 1):
                    reciprocal_std(B - 1, t)
                for t in (2 * g, 2 * g + 1):
                    scale_shift(B - 1, t, final=True)


def group_columns(g):
    p, h = divmod(g, NT // 2)
    return p, h * GW, GW if h + 1 < NT // 2 else GW - (TT - LAST)


class Before:
    def __init__(self, im):
        self.b = im.b - 1


_INS = ["x", "L0_conv_wq", "L0_conv_bq", "L0_conv_wk", "L0_conv_bk", "L0_conv_wv", "L0_conv_bv", "L0_conv_wo",
        "L0_conv_bo", "L0_conv_ln_gamma", "L0_conv_ln_beta", "L0_conv_spatial_bias"]


def kernel(**inputs):
    import numpy as _np
    import concourse.bacc as _bacc
    from concourse import mybir as _mybir
    from concourse.bass_utils import run_bass_kernel_spmd as _run

    nc = _bacc.Bacc("TRN2", target_bir_lowering=False, num_devices=1)
    arrays, args = {}, []
    for name in _INS:
        a = _np.ascontiguousarray(inputs[name])
        arrays[f"in_{name}"] = a
        args.append(nc.dram_tensor(f"in_{name}", a.shape, _mybir.dt.from_np(a.dtype), kind="ExternalInput").ap())
    out = nc.dram_tensor("out", (B, GRID, GRID, D), _mybir.dt.float32, kind="ExternalOutput").ap()
    attention_layernorm(nc, *args, out)
    r = _run(nc, [arrays], core_ids=[0])
    return r.results[0]["out"]
```
